# Optimizing a Trainium2 kernel written in Bass

```python
import numpy as np
import jax
import jax.numpy as jnp

def _softmax(x, axis=-1):
    return jax.nn.softmax(x, axis=axis)

def _gelu(x):
    return jax.nn.gelu(x, approximate=True)

def _silu(x):
    return jax.nn.silu(x)

def _sigmoid(x):
    return jax.nn.sigmoid(x)

def _layernorm(x, axis=-1, eps=1e-05):
    m = jnp.mean(x, axis=axis, keepdims=True)
    v = jnp.var(x, axis=axis, keepdims=True)
    return (x - m) / jnp.sqrt(v + eps)

def _scatter_add(tgt, idx, src, axis=0):
    return tgt.at[idx].add(src)

def _segment_sum(src, seg, n):
    return jax.ops.segment_sum(src, seg, n)
kernel_name = 'mk_seq_postln_d1_jaxref_r8_d7400a'

def setup_inputs(seed: int=0):
    np.random.seed(seed)
    _w = jnp.asarray

    def _L0_attn_setup():
        import jax, jax.numpy as jnp
        import numpy as np
        B, N, D, H = (8, 128, 128, 16)
        HD = D // H
        SCALE = HD ** (-0.5)
        key = jax.random.key(seed)
        k1, k2, k3, k4, k5 = jax.random.split(key, 5)
        return {'x': jax.random.normal(k1, (B, N, D), dtype=jnp.float32), 'qkv_w': jax.random.normal(k2, (3 * D, D), dtype=jnp.float32) * 0.02, 'qkv_b': jax.random.normal(k3, (3 * D,), dtype=jnp.float32) * 0.02, 'fc_w': jax.random.normal(k4, (D, D), dtype=jnp.float32) * 0.02, 'fc_b': jax.random.normal(k5, (D,), dtype=jnp.float32) * 0.02}
    _L0_attn_in = _L0_attn_setup()

    def _L0_ffn_setup():
        import jax, jax.numpy as jnp
        import numpy as np
        D_IN, D_HID = (128, 512)

        def _ternary(key, shape):
            return jax.random.randint(key, shape, -1, 2).astype(jnp.float32)

        def _tlin(x, w, s):
            return jnp.einsum('bsi,oi->bso', x, w) * s
        key = jax.random.key(seed)
        ks = jax.random.split(key, 12)
        inv = lambda fan: 1.0 / np.sqrt(fan).astype(np.float32)
        return {'x': jax.random.normal(ks[0], (4, 256, D_IN), dtype=jnp.float32), 'w1_w': _ternary(ks[1], (D_HID, D_IN)), 'w1_s': jax.random.uniform(ks[2], (D_HID,), dtype=jnp.float32) * inv(D_IN), 'w2_w': _ternary(ks[3], (D_HID, D_IN)), 'w2_s': jax.random.uniform(ks[4], (D_HID,), dtype=jnp.float32) * inv(D_IN), 'h1_w': _ternary(ks[5], (D_HID, D_HID)), 'h1_s': jax.random.uniform(ks[6], (D_HID,), dtype=jnp.float32) * inv(D_HID), 'h2_w': _ternary(ks[7], (D_HID, D_HID)), 'h2_s': jax.random.uniform(ks[8], (D_HID,), dtype=jnp.float32) * inv(D_HID), 'w3_w': _ternary(ks[9], (D_IN, D_HID)), 'w3_s': jax.random.uniform(ks[10], (D_IN,), dtype=jnp.float32) * inv(D_HID)}
    _L0_ffn_in = _L0_ffn_setup()
    _d = {'L0_attn_x': _L0_attn_in['x'], 'L0_attn_qkv_w': _L0_attn_in['qkv_w'], 'L0_attn_qkv_b': _L0_attn_in['qkv_b'], 'L0_attn_fc_w': _L0_attn_in['fc_w'], 'L0_attn_fc_b': _L0_attn_in['fc_b'], 'L0_ffn_w1_w': _L0_ffn_in['w1_w'], 'L0_ffn_w1_s': _L0_ffn_in['w1_s'], 'L0_ffn_w2_w': _L0_ffn_in['w2_w'], 'L0_ffn_w2_s': _L0_ffn_in['w2_s'], 'L0_ffn_h1_w': _L0_ffn_in['h1_w'], 'L0_ffn_h1_s': _L0_ffn_in['h1_s'], 'L0_ffn_h2_w': _L0_ffn_in['h2_w'], 'L0_ffn_h2_s': _L0_ffn_in['h2_s'], 'L0_ffn_w3_w': _L0_ffn_in['w3_w'], 'L0_ffn_w3_s': _L0_ffn_in['w3_s']}
    _x0 = _d['L0_attn_x']
    _d['L0_attn_x'] = jax.random.normal(jax.random.fold_in(jax.random.key(seed), 1), (4, 512, 128), dtype=_x0.dtype)
    del _x0
    return _d

def reference(L0_attn_x, L0_attn_qkv_w, L0_attn_qkv_b, L0_attn_fc_w, L0_attn_fc_b, L0_ffn_w1_w, L0_ffn_w1_s, L0_ffn_w2_w, L0_ffn_w2_s, L0_ffn_h1_w, L0_ffn_h1_s, L0_ffn_h2_w, L0_ffn_h2_s, L0_ffn_w3_w, L0_ffn_w3_s):

    def _L0_attn_ref(x, qkv_w, qkv_b, fc_w, fc_b):
        import jax, jax.numpy as jnp
        import numpy as np
        B, N, D, H = (8, 128, 128, 16)
        HD = D // H
        SCALE = HD ** (-0.5)
        b, n, d = x.shape
        qkv = (jnp.einsum('bnd,ed->bne', x, qkv_w) + qkv_b).reshape(b, n, H, 3 * HD)
        q, k, v = jnp.split(qkv, 3, axis=-1)
        q = q.transpose(0, 2, 1, 3)
        k = k.transpose(0, 2, 1, 3)
        v = v.transpose(0, 2, 1, 3)
        attn = jax.nn.softmax(jnp.einsum('bhqd,bhkd->bhqk', q, k) * SCALE, axis=-1)
        out = jnp.einsum('bhqk,bhkd->bhqd', attn, v)
        out = out.transpose(0, 2, 1, 3).reshape(b, n, d)
        return jnp.einsum('bnd,ed->bne', out, fc_w) + fc_b + x

    def _L0_ffn_ref(x, w1_w, w1_s, w2_w, w2_s, h1_w, h1_s, h2_w, h2_s, w3_w, w3_s):
        import jax, jax.numpy as jnp
        import numpy as np
        D_IN, D_HID = (128, 512)

        def _ternary(key, shape):
            return jax.random.randint(key, shape, -1, 2).astype(jnp.float32)

        def _tlin(x, w, s):
            return jnp.einsum('bsi,oi->bso', x, w) * s
        h = jax.nn.silu(_tlin(x, w1_w, w1_s)) * _tlin(x, w2_w, w2_s)
        h = jax.nn.gelu(_tlin(h, h1_w, h1_s), approximate=False)
        h = jax.nn.gelu(_tlin(h, h2_w, h2_s), approximate=False)
        return _tlin(h, w3_w, w3_s)
    x = L0_attn_x
    x = _layernorm(x + _L0_attn_ref(x, L0_attn_qkv_w, L0_attn_qkv_b, L0_attn_fc_w, L0_attn_fc_b), axis=-1)
    x = _layernorm(x + _L0_ffn_ref(x, L0_ffn_w1_w, L0_ffn_w1_s, L0_ffn_w2_w, L0_ffn_w2_s, L0_ffn_h1_w, L0_ffn_h1_s, L0_ffn_h2_w, L0_ffn_h2_s, L0_ffn_w3_w, L0_ffn_w3_s), axis=-1)
    return x

_drawn_inputs = setup_inputs


def setup_inputs(seed=0):
    import zlib

    import numpy as np

    out = dict(_drawn_inputs(seed))
    spreads = {}
    factors = {'L0_attn_qkv_w': 8.0,
     'L0_attn_qkv_b': 8.0,
     'L0_attn_fc_w': 8.0,
     'L0_attn_fc_b': 5.495,
     'L0_ffn_w1_w': 8.0,
     'L0_ffn_w1_s': 8.0,
     'L0_ffn_w2_w': 8.0,
     'L0_ffn_w2_s': 8.0,
     'L0_ffn_h1_w': 8.0,
     'L0_ffn_h1_s': 8.0,
     'L0_ffn_h2_w': 8.0,
     'L0_ffn_h2_s': 8.0,
     'L0_ffn_w3_w': 8.0,
     'L0_ffn_w3_s': 8.0}
    for name, (base, spread) in spreads.items():
        noise = np.random.default_rng([zlib.crc32(name.encode()), seed]).standard_normal(out[name].shape)
        drawn = base * np.exp(spread * noise) if base else spread * noise
        out[name] = jnp.asarray(drawn.astype(out[name].dtype))
    for name, factor in factors.items():
        out[name] = (out[name] * factor).astype(out[name].dtype)
    return out
```

```python
import numpy as np

import concourse.bass as bass
from concourse import mybir
from contextlib import ExitStack


def post_ln_block_kernel(
    nc: bass.Bass,
    x: bass.AP,
    qkv_w: bass.AP,
    qkv_b: bass.AP,
    fc_w: bass.AP,
    fc_b: bass.AP,
    w1_w: bass.AP,
    w1_s: bass.AP,
    w2_w: bass.AP,
    w2_s: bass.AP,
    h1_w: bass.AP,
    h1_s: bass.AP,
    h2_w: bass.AP,
    h2_s: bass.AP,
    w3_w: bass.AP,
    w3_s: bass.AP,
    out: bass.AP,
):
    F32, F32R, BF16 = mybir.dt.float32, mybir.dt.float32r, mybir.dt.bfloat16
    ALU = mybir.AluOpType
    ACT = mybir.ActivationFunctionType
    AX = mybir.AxisListType

    P = 128
    B, N, D = x.shape
    H = 16
    HD = D // H
    HID = w1_w.shape[0]
    SCALE = float(HD) ** -0.5
    EPS = 1e-5
    NT = N // P
    NK = HID // P
    GH = 4
    NG = H // GH
    GT = GH * NT
    BT = NG * GT
    NPART = 3
    SLOTS = 6
    SR = SLOTS * HD
    MROW = 96
    VW = 32
    LEAD = 26
    TWO_ONES = float(np.array([0x3F803F80], np.uint32).view(np.float32)[0])
    NP = 8
    assert D == P and HID == 512 and N == 512 and H == 16

    with ExitStack() as ctx:
        def sb(name, shape, dt):
            return ctx.enter_context(nc.sbuf_tensor(name, shape, dt))

        def sem(name):
            return ctx.enter_context(nc.semaphore(name))

        def bank(name):
            return ctx.enter_context(nc.psum_tensor(name, [P, 512], F32))

        s_bank = [bank(f"s_bank{i}") for i in range(2)]
        st_bank = [bank(f"st_bank{i}") for i in range(2)]
        pv_bank = bank("pv_bank")
        t_bank = bank("t_bank")
        f_bank = [bank(f"f_bank{i}") for i in range(2)]
        t_bank16 = t_bank[:, :].bitcast(BF16)

        ident = sb("ident", [P, P], F32)
        ident16 = sb("ident16", [P, P], BF16)
        h1_nat = sb("h1_nat", [P, NK, HID], F32)
        work = sb("work", [P, 6, N], F32)
        y = sb("y", [P, NT, D], F32)
        res = sb("res", [P, NT, D], F32)
        qkv_nat, fc_nat = res[:, 0:3, :], res[:, 3, :]
        h_nat = [h1_nat[:, :, :], work[:, 0:4, :]]
        w_nat = work[:, 4:6, :].rearrange("p w (t c) -> p w t c", t=NK)
        w3_nat = y[:, :, :].rearrange("p t c -> p (t c)")
        qkvT = sb("qkvT", [P, 3, D], F32)
        fcT = sb("fcT", [P, D], F32)
        w12T = [sb(f"w12T{i}", [P, 2, HID], F32R) for i in range(2)]
        hT = [sb(f"hT{i}", [P, 2 * NK, HID], F32R) for i in range(2)]
        w3T = [sb(f"w3T{i}", [P, NK, D], F32R) for i in range(2)]
        qkb = sb("qkb", [P, 2], F32)
        vb = sb("vb", [P, NT, D], F32)
        fcb = sb("fcb", [P, NT, D], F32)
        s3 = sb("s3", [P, NT, D], F32)
        hs = sb("hs", [P, 4, NK], F32)

        x_in = sb("x_in", [P, NT, D], F32)
        x_res = sb("x_res", [P, NT, D], F32)
        xT = sb("xT", [P, N], F32)
        qk_f = [sb(f"qk_f{i}", [P, N], F32) for i in range(2)]
        qk_r = [sb(f"qk_r{i}", [P, N], F32) for i in range(2)]
        parts = [sb(f"parts{i}", [P, SLOTS, N], BF16) for i in range(2)]
        stack = [sb(f"stack{i}", [P, H, N], BF16) for i in range(2)]
        v_sb = sb("v_sb", [P, NT, H, VW], F32)
        negmax = sb("negmax", [P, 2, NT, GH], F32)
        mres = sb("mres", [P, NT, GH], F32)
        mparts = sb("mparts", [P, NT, NPART, GH], BF16)
        mT = sb("mT", [GH * NPART, N], BF16)
        prob = sb("prob", [P, NP, N], F32)
        oT = sb("oT", [P, N], F32)
        rden = sb("rden", [P, NT * GH], F32)
        attn = sb("attn", [P, NT, D], F32)
        aT = sb("aT", [P, N], F32)
        stats = sb("stats", [P, NT, 6], F32)
        mv = sb("mv", [P, NT, 2], F32)
        rstd = sb("rstd", [P, 2, NT], F32)
        mhalf = sb("mhalf", [P, NT], F32)
        x1 = sb("x1", [P, NT, D], F32)
        x1T = [sb(f"x1T{i}", [P, N], F32R) for i in range(2)]
        silu, hf, gf = work[:, 0:2, :], work[:, 2:4, :], work[:, 4:6, :]
        act0 = [sb(f"act0_{i}", [P, NK, N], F32R) for i in range(2)]
        act1 = [sb(f"act1_{i}", [P, NK, N], F32R) for i in range(2)]
        act2 = act0

        ld_qkv, ld_bias, ld_x, ld_res, ld_w, ld_h, ld_w3, ld_s = (
            sem(n) for n in ("ld_qkv", "ld_bias", "ld_x", "ld_res", "ld_w", "ld_h", "ld_w3", "ld_s"))
        st_out = sem("st_out")
        ids, ones, zeros, vzero = sem("ids"), sem("ones"), sem("zeros"), sem("vzero")
        ps_wq, ev_wq = sem("ps_wq"), sem("ev_wq")
        ps_wt, hi_wt, ev_wt = sem("ps_wt"), sem("hi_wt"), sem("ev_wt")
        ps_xT, ev_xT = sem("ps_xT"), sem("ev_xT")
        ps_qk, ev_qk, qk_a, qk_step, qk_parts = (
            sem(n) for n in ("ps_qk", "ev_qk", "qk_a", "qk_step", "qk_parts"))
        ps_v, ev_v = sem("ps_v"), sem("ev_v")
        rep = [sem(f"rep{j}") for j in range(NG)]
        ps_s, ev_s = sem("ps_s"), sem("ev_s")
        m_step, m_parts, ps_mT, ev_mT = (sem(n) for n in ("m_step", "m_parts", "ps_mT", "ev_mT"))
        mrow = [sem(f"mrow{j}") for j in range(NG)]
        ps_st, ev_st, ps_pv = sem("ps_st"), sem("ev_st"), sem("ps_pv")
        ev_pv, ps_oT, rd_oT, ev_oT = (sem(n) for n in ("ev_pv", "ps_oT", "rd_oT", "ev_oT"))
        ps_aT, ev_aT, ps_fc = (sem(n) for n in ("ps_aT", "ev_aT", "ps_fc"))
        res2, resb = sem("res2"), sem("resb")
        rs_ok = sem("rs_ok")
        ln_step, x1_ok, y_ok = sem("ln_step"), sem("x1_ok"), sem("y_ok")
        ps_x1T, hi_x1T, ev_x1T = sem("ps_x1T"), sem("hi_x1T"), sem("ev_x1T")
        ps_w1, ps_w2, ev_w1, ev_w2 = (sem(n) for n in ("ps_w1", "ps_w2", "ev_w1", "ev_w2"))
        hi0, lo0 = sem("hi0"), sem("lo0")
        ps_h, ev_h, hi_g, lo_g = (sem(n) for n in ("ps_h", "ev_h", "hi_g", "lo_g"))
        ps_w3, ev_w3 = sem("ps_w3"), sem("ev_w3")

        def wait(eng, s, value):
            if not isinstance(value, int) or value > 0:
                eng.wait_ge(s, value)

        WT = 3 + 2 * NK

        def order(s):
            now, nxt, prev = s < B, s + 1 < B, s >= 1
            items = []

            def add(cost, *item):
                items.append((cost, item))

            wt = list(range(WT)) if s == 0 else []
            for j in range(NG):
                for i in range(GT):
                    if now:
                        add(0.22, "st", j, i)
                    if s == 0 and i % 2 == 0 and wt:
                        add(0.44, "wt", wt.pop(0))
                    if i == 3 and (j or prev) and (now or j == 0):
                        add(0.9, "pv", j - 1, 3)
                    if i == 5 and (j or prev) and (now or j == 0):
                        add(0, "oT_in", j - 1)
                    if now and i in (7, 11, 15):
                        add(0.9, "pv", j, (i - 7) // 4)
                    if i == 8 and (j or prev) and (now or j == 0):
                        add(0.44, "oT", j - 1)
                    if prev and j == 0 and i == 11:
                        add(0.44, "aT")
                    if now and i == 13 and (j < NG - 1 or nxt):
                        add(0.22, "mT", j + 1)
                    if prev and now and j == 0 and i == 5:
                        add(0.9, "v")
                    if prev and j == 0 and i == 14:
                        add(0.9, "fc")
                    if prev and j == 1 and i == 3:
                        add(0.44, "x1T")
                    if nxt and j == 1 and i == 5:
                        add(0.44, "xT")
                    if prev and j == 1 and i == 6:
                        for k in range(NK):
                            add(0.86, "w12", k)
                    if nxt and j == 1 and i == 12:
                        add(0.9, "qk", 0)
                        add(0.9, "qk", 1)
                    if prev and j == 2 and i == 1:
                        for k in range(NK):
                            add(1.73, "h", 0, k)
                    if prev and j == 3 and i == 1:
                        for k in range(NK):
                            add(1.73, "h", 1, k)
                    if prev and j == 3 and i == 11:
                        add(2.5, "w3")
            if not now:
                return [it for _, it in items]
            first = GT if s == 0 else LEAD
            tiles = BT + LEAD - first
            total = sum(c for c, _ in items)
            res_, t, r = [], 0.0, 0
            for c, it in items:
                while r < tiles and t >= total * r / tiles:
                    if s * BT + first + r < B * BT:
                        res_.append(("s", first + r))
                    r += 1
                if it[0] == "mT":
                    while first + r < (it[1] + 1) * GT and r < tiles:
                        res_.append(("s", first + r))
                        r += 1
                res_.append(it)
                t += c
            while r < tiles and s * BT + first + r < B * BT:
                res_.append(("s", first + r))
                r += 1
            return res_

        def prologue():
            return [("xT",), ("qk", 0), ("qk", 1)] + [("s", m) for m in range(GT)] + [("v",), ("mT", 0)]

        def program():
            for it in prologue():
                yield -1, it
            for s in range(B + 1):
                for it in order(s):
                    yield s, it

        block = ctx.enter_context(nc.Block())

        @block.sync
        def _(sp):
            sp.dma_start(qkv_nat, qkv_w.rearrange("(t p) c -> p t c", p=P)).then_inc(ld_qkv, 16)
            sp.dma_start(x_in[:, :, :], x[0].rearrange("(t p) c -> p t c", p=P)).then_inc(ld_x, 16)
            qkv_bh = qkv_b.rearrange("(h k d) -> k h d", k=3, d=HD)
            for i in range(2):
                sp.dma_start(qkb[:, i:i + 1], qkv_bh[i]).then_inc(ld_bias, 16)
            sp.dma_start(fc_nat, fc_w).then_inc(ld_qkv, 16)
            for t in range(NT):
                sp.dma_start(vb[:, t, :].rearrange("p (h d) -> p h d", d=HD),
                             qkv_bh[2].partition_broadcast(P)).then_inc(ld_bias, 16)
                sp.dma_start(fcb[:, t, :], fc_b.partition_broadcast(P)).then_inc(ld_bias, 16)
                sp.dma_start(s3[:, t, :], w3_s.partition_broadcast(P)).then_inc(ld_s, 16)
            for i, w in enumerate((w1_s, w2_s, h1_s, h2_s)):
                sp.dma_start(hs[:, i, :], w.rearrange("(k p) -> p k", p=P),
                             allow_slow_non_contiguous=True).then_inc(ld_s, 16)
            for i, w in enumerate((w1_w, w2_w)):
                sp.dma_start(w_nat[:, i, :, :], w.rearrange("(t p) c -> p t c", p=P)).then_inc(ld_w, 16)
            for i, w in enumerate((h1_w, h2_w)):
                sp.dma_start(h_nat[i], w.rearrange("(t p) c -> p t c", p=P)).then_inc(ld_h, 16)
            sp.dma_start(w3_nat, w3_w).then_inc(ld_w3, 16)
            sp.dma_start(x_res[:, :, :], x[0].rearrange("(t p) c -> p t c", p=P)).then_inc(ld_res, 16)

            def spread(b, j):
                wait(sp, qk_parts, 2 * (b + 1))
                if b == 0 and j == 0:
                    wait(sp, ones, 3)
                    wait(sp, zeros, 2)
                wait(sp, ps_st, BT * (b - 1) + GT * (j + 1))
                for h in range(GH * j, GH * (j + 1)):
                    for i in range(2):
                        sp.dma_start(stack[i][0:SR, h, :],
                                     parts[i][HD * h:HD * h + HD, :, :]).then_inc(rep[j], 16)

            for s, it in program():
                b = s + 1
                if it == ("qk", 1):
                    spread(b, 0)
                    if b == 0:
                        for j in range(1, NG):
                            spread(b, j)
                    if b + 1 < B:
                        wait(sp, ps_xT, b + 1)
                        sp.dma_start(x_in[:, :, :], x[b + 1].rearrange("(t p) c -> p t c", p=P)).then_inc(ld_x, 16)
                if it[0] == "st" and it[2] == 0 and it[1] >= 2 and s + 1 < B:
                    spread(s + 1, it[1] - 1)
                if it == ("pv", -1, 3) and 1 <= s < B:
                    spread(s, NG - 1)
                if it[0] == "mT":
                    g = NG * s + it[1] if s >= 0 else 0
                    wait(sp, ev_mT, g + 1)
                    j = it[1] % NG
                    sp.dma_start(stack[0][MROW:MROW + NPART, GH * j:GH * (j + 1), :], mT[:, :]).then_inc(mrow[j], 16)
                if it == ("fc",) and s < B:
                    wait(sp, ln_step, 8 * (s - 1) + 1)
                    sp.dma_start(x_res[:, :, :], x[s].rearrange("(t p) c -> p t c", p=P)).then_inc(ld_res, 16)
                if it == ("w3",):
                    wait(sp, y_ok, s)
                    sp.dma_start(out[s - 1].rearrange("(t p) c -> p t c", p=P), y[:, :, :]).then_inc(st_out, 16)
            sp.wait_ge(st_out, 16 * B)

        @block.tensor
        def _(pe):
            def transpose4(dst, src):
                for t in range(4):
                    last = nc.tensor.transpose(dst[:, t * P:(t + 1) * P], src(t), ident[:, :])
                return last

            pe.wait_ge(ids, 4)
            pe.wait_ge(ld_qkv, 32)
            for t in range(3):
                nc.tensor.transpose(f_bank[0][:, t * P:(t + 1) * P], qkv_nat[:, t, :], ident[:, :])
            nc.tensor.transpose(f_bank[0][:, 3 * P:4 * P], fc_nat, ident[:, :]).then_inc(ps_wq, 1)

            def scores_q(m, b):
                j, c, qt = m // GT, (m % GT) // NT, m % NT
                h = GH * j + c
                if m % GT == 0:
                    wait(pe, rep[j], 16 * 2 * GH * (b + 1))
                wait(pe, ev_s, b * BT + m - 1)
                nc.tensor.matmul(s_bank[m % 2][:, :], stack[0][0:MROW, h, qt * P:(qt + 1) * P],
                                 stack[1][0:MROW, h, :], start=True, stop=True).then_inc(ps_s, 1)

            def scores_k(n, b):
                j, kt, c = n // GT, (n % GT) // GH, n % GH
                h = GH * j + c
                if n % GT == 0:
                    wait(pe, mrow[j], 16 * (b + 1))
                wait(pe, ev_st, b * BT + n - 1)
                nc.tensor.matmul(st_bank[n % 2][:, :], stack[1][:, h, kt * P:(kt + 1) * P], stack[0][:, h, :], start=True, stop=True).then_inc(ps_st, 1)

            def pv(g, kt):
                wait(pe, ev_st, (NT * g + kt + 1) * GH)
                if kt == 0:
                    wait(pe, ev_pv, g)
                    wait(pe, ev_v, g // NG + 1)
                j = g % NG
                for c in range(GH):
                    last = nc.tensor.matmul(pv_bank[VW * c:VW * c + VW, :], v_sb[:, kt, GH * j + c, :],
                                            prob[:, (GH * kt + c) % NP, :], start=kt == 0, stop=kt == NT - 1)
                last.then_inc(ps_pv, 1)

            def split_mm(dst, wt, xs, first, last):
                n = 0
                for w in wt:
                    for v in xs:
                        mm = nc.tensor.matmul(dst, w, v, start=first and n == 0, stop=last and n == 3)
                        n += 1
                return mm

            for s, it in program():
                what = it[0]
                if what == "s":
                    m = it[1]
                    scores_q(m % BT, max(s, 0) + m // BT)
                elif what == "st":
                    scores_k(GT * it[1] + it[2], s)
                elif what == "pv":
                    pv(NG * s + it[1], it[2])
                elif what == "xT":
                    b = s + 1
                    wait(pe, ld_x, 16 * (b + 1))
                    if s >= 1:
                        wait(pe, ev_x1T, s)
                    elif s == 0:
                        wait(pe, ev_mT, 2)
                    transpose4(t_bank, lambda t: x_in[:, t, :]).then_inc(ps_xT, 1)
                elif what == "qk":
                    b, i = s + 1, it[1]
                    wait(pe, ev_xT, b + 1)
                    if s == -1:
                        wait(pe, ev_wq, 4)
                    elif s == 0:
                        wait(pe, ev_wt, WT)
                    else:
                        wait(pe, (ev_w1, ev_w2)[i], NK * s)
                    nc.tensor.matmul(f_bank[i][:, :], qkvT[:, i, :], xT[:, :], start=True, stop=True).then_inc(ps_qk, 1)
                elif what == "v":
                    b = max(s, 0)
                    wait(pe, ev_xT, b + 1)
                    if s >= 2:
                        wait(pe, ev_w3, s - 1)
                    else:
                        wait(pe, ev_qk, 2 * b + 1)
                    for t in range(NT):
                        last = nc.tensor.matmul(f_bank[0][:, t * P:(t + 1) * P], xT[:, t * P:(t + 1) * P],
                                                qkvT[:, 2, :], start=True, stop=True)
                    last.then_inc(ps_v, 1)
                elif what == "mT":
                    g = NG * s + it[1] if s >= 0 else 0
                    wait(pe, m_parts, g + 1)
                    if s == -1:
                        wait(pe, ev_xT, 1)
                    elif it[1] == 1 and s >= 1:
                        wait(pe, ev_aT, s)
                    elif g >= 2:
                        wait(pe, ev_oT, g - 1)
                    for t in range(NT):
                        last = nc.tensor.transpose(t_bank16[0:GH * NPART, t * P:(t + 1) * P],
                                                   mparts[:, t, :, :].rearrange("p m c -> p (m c)"), ident16[:, :])
                    last.then_inc(ps_mT, 1)
                elif what == "oT":
                    g = NG * s + it[1]
                    wait(pe, ev_pv, g + 1)
                    if it[1] == 0 and s + 1 < B:
                        wait(pe, ev_xT, s + 2)
                    elif it[1] == 0:
                        wait(pe, ev_x1T, s)
                    elif g + 1 < NG * B:
                        wait(pe, ev_mT, g + 2)
                    else:
                        wait(pe, ev_oT, g)
                    transpose4(t_bank, lambda t: oT[:, t * P:(t + 1) * P]).then_inc(ps_oT, 1)
                elif what == "aT":
                    wait(pe, ev_oT, NG * s)
                    transpose4(t_bank, lambda t: attn[:, t, :]).then_inc(ps_aT, 1)
                elif what == "fc":
                    wait(pe, ev_aT, s)
                    if s == 1:
                        wait(pe, ev_qk, 4)
                    else:
                        wait(pe, ev_h, 2 * NK * (s - 1))
                    for t in range(NT):
                        last = nc.tensor.matmul(f_bank[1][:, t * P:(t + 1) * P], aT[:, t * P:(t + 1) * P],
                                                fcT[:, :], start=True, stop=True)
                    last.then_inc(ps_fc, 1)
                elif what == "x1T":
                    wait(pe, x1_ok, s)
                    if s < B:
                        wait(pe, ev_mT, NG * s + 2)
                    else:
                        wait(pe, ev_aT, s)
                    transpose4(t_bank, lambda t: x1[:, t, :]).then_inc(ps_x1T, 1)
                elif what == "w12":
                    k = it[1]
                    cols = slice(k * P, (k + 1) * P)
                    if k == 0:
                        wait(pe, ev_x1T, s)
                        wait(pe, ev_wt, WT)
                        wait(pe, ln_step, 8 * (s - 1) + 1)
                        if s < B:
                            wait(pe, ev_v, s + 1)
                        else:
                            wait(pe, ev_w3, s - 1)
                    else:
                        wait(pe, ev_w1, NK * (s - 1) + k)
                    xs = [x1T[0][:, :], x1T[1][:, :]]
                    split_mm(f_bank[0][:, :], [w[:, 0, cols] for w in w12T], xs, True, True).then_inc(ps_w1, 1)
                    if k:
                        wait(pe, ev_w2, NK * (s - 1) + k)
                    split_mm(f_bank[1][:, :], [w[:, 1, cols] for w in w12T], xs, True, True).then_inc(ps_w2, 1)
                elif what == "h":
                    layer, k = it[1], it[2]
                    cols = slice(k * P, (k + 1) * P)
                    done = NK * (2 * (s - 1) + layer)
                    src = (act0, act1)[layer]
                    if k == 0:
                        wait(pe, hi0 if layer == 0 else hi_g, (NK * s) if layer == 0 else done)
                        wait(pe, lo0 if layer == 0 else lo_g, (NK * s) if layer == 0 else done)
                    if layer == 0 and k < 2:
                        if s + 1 < B:
                            wait(pe, ev_qk, 2 * (s + 1) + k + 1)
                        else:
                            wait(pe, (ev_w1, ev_w2)[k], NK * s)
                    else:
                        wait(pe, ev_h, done + k - 1)
                    for kk in range(NK):
                        last = split_mm(f_bank[k % 2][:, :], [w[:, NK * layer + kk, cols] for w in hT],
                                        [a[:, kk, :] for a in src], kk == 0, kk == NK - 1)
                    last.then_inc(ps_h, 1)
                elif what == "w3":
                    wait(pe, hi_g, 2 * NK * s)
                    wait(pe, lo_g, 2 * NK * s)
                    wait(pe, ev_h, 2 * NK * s - 1)
                    for t in range(NT):
                        for kk in range(NK):
                            last = split_mm(f_bank[0][:, t * P:(t + 1) * P],
                                            [a[:, kk, t * P:(t + 1) * P] for a in act2],
                                            [w[:, kk, :] for w in w3T], kk == 0, kk == NK - 1)
                    last.then_inc(ps_w3, 1)
                elif what == "wt":
                    u = it[1]
                    if u == 0:
                        wait(pe, ev_v, 1)
                        wait(pe, ev_qk, 2)
                    wait(pe, ev_wt, u - 1)
                    bank_ = f_bank[u % 2]
                    if u < 2:
                        wait(pe, ld_w, 32)
                        last = transpose4(bank_, lambda t: w_nat[:, u, t, :])
                    elif u < 2 + 2 * NK:
                        wait(pe, ld_h, 32)
                        layer, kk = (u - 2) // NK, (u - 2) % NK
                        last = transpose4(bank_, lambda t: h_nat[layer][:, t, kk * P:(kk + 1) * P])
                    else:
                        wait(pe, ld_w3, 16)
                        last = transpose4(bank_, lambda t: w3_nat[:, t * P:(t + 1) * P])
                    last.then_inc(ps_wt, 1)

        def wt_dst(u, part):
            if u < 2:
                return w12T[part][:, u, :]
            if u < 2 + 2 * NK:
                return hT[part][:, u - 2, :]
            return w3T[part][:, :, :].rearrange("p k c -> p (k c)")

        @block.scalar
        def _(act):
            act.wait_ge(ld_bias, 16 * (2 + 2 * NT))
            for s, it in program():
                what = it[0]
                if what == "st":
                    r = GT * it[1] + it[2]
                    n = BT * s + r
                    if n % GH == 0:
                        wait(act, ps_pv, n // GH - 1)
                    act.wait_ge(ps_st, n + 1)
                    nc.scalar.activation(prob[:, r % NP, :], st_bank[r % 2][:, :], ACT.Exp, scale=SCALE).then_inc(ev_st, 1)
                elif what == "xT":
                    act.wait_ge(ps_xT, s + 2)
                    if s >= 0:
                        act.wait_ge(ps_v, s + 1)
                    nc.scalar.activation(xT[:, :], t_bank[:, :], ACT.Copy).then_inc(ev_xT, 1)
                elif what == "qk":
                    b, i = s + 1, it[1]
                    act.wait_ge(ps_qk, 2 * b + i + 1)
                    wait(act, qk_parts, 2 * (b - 1) + i + 1)
                    nc.scalar.activation(qk_f[i][:, :], f_bank[i][:, :], ACT.Identity, bias=qkb[:, i:i + 1]).then_inc(ev_qk, 1)
                elif what == "mT":
                    g = NG * s + it[1] if s >= 0 else 0
                    act.wait_ge(ps_mT, g + 1)
                    if g:
                        act.wait_ge(mrow[(g - 1) % NG], 16 * ((g - 1) // NG + 1))
                    nc.scalar.activation(mT[:, :], t_bank16[0:GH * NPART, 0:N], ACT.Copy).then_inc(ev_mT, 1)
                elif what == "oT_in":
                    g = NG * s + it[1]
                    act.wait_ge(ps_pv, NT * (g + 1))
                    wait(act, ps_oT, g)
                    nc.scalar.activation(oT[:, :], pv_bank[:, :], ACT.Copy).then_inc(ev_pv, 1)
                elif what == "aT":
                    act.wait_ge(ps_aT, s)
                    wait(act, ps_fc, s - 1)
                    nc.scalar.activation(aT[:, :], t_bank[:, :], ACT.Copy).then_inc(ev_aT, 1)
                elif what == "w12":
                    k = it[1]
                    n = NK * (s - 1) + k
                    if n == 0:
                        act.wait_ge(ld_s, 16 * (NT + 4))
                    act.wait_ge(ps_w1, n + 1)
                    wait(act, ev_w2, n - 1)
                    nc.scalar.activation(silu[:, k % 2, :], f_bank[0][:, :], ACT.Silu, scale=hs[:, 0, k:k + 1]).then_inc(ev_w1, 1)
                elif what == "h":
                    layer, k = it[1], it[2]
                    n = NK * (2 * (s - 1) + layer) + k
                    act.wait_ge(ps_h, n + 1)
                    wait(act, lo_g, n - 1)
                    nc.scalar.activation(gf[:, k % 2, :], f_bank[k % 2][:, :], ACT.Gelu, scale=hs[:, 2 + layer, k:k + 1]).then_inc(ev_h, 1)
                elif what == "wt":
                    u = it[1]
                    act.wait_ge(ps_wt, u + 1)
                    nc.scalar.activation(wt_dst(u, 0), f_bank[u % 2][:, :], ACT.Copy).then_inc(hi_wt, 1)

        @block.vector
        def _(dve):
            k_rows = stack[1][:, :, :].rearrange("p h n -> p (h n)").bitcast(F32)
            nc.vector.memset(k_rows[32:64, :], 0.0).then_inc(ones, 1)
            nc.vector.memset(k_rows[64:MROW, :], 0.0).then_inc(ones, 1)
            nc.vector.memset(k_rows[MROW:P, :], TWO_ONES).then_inc(ones, 1)
            dve.wait_ge(ps_wq, 1)
            for i in range(3):
                nc.vector.tensor_copy(qkvT[:, i, :].rearrange("p (h d) -> p h d", d=HD),
                                      f_bank[0][:, 0:3 * D].rearrange("p (h k d) -> p k h d", k=3, d=HD)[:, i]).then_inc(ev_wq, 1)
            nc.vector.tensor_copy(fcT[:, :], f_bank[0][:, 3 * D:4 * D]).then_inc(ev_wq, 1)
            dve.wait_ge(ld_bias, 16 * (2 + 2 * NT))

            def layernorm(count, dst, done):
                dve.wait_ge(ln_step, 4 * count + 1)
                for t in range(NT):
                    last = nc.vector.bn_stats(stats[:, t, :], res[:, t, :])
                last.then_inc(ln_step, 1)
                dve.wait_ge(ln_step, 4 * count + 2)
                for t in range(NT):
                    last = nc.vector.bn_aggr(mv[:, t, :], stats[:, t, :])
                last.then_inc(ln_step, 1)
                dve.wait_ge(ln_step, 4 * count + 3)
                nc.vector.tensor_scalar(rstd[:, 0, :], mv[:, :, 1], EPS, None, ALU.add).then_inc(ln_step, 1)
                dve.wait_ge(rs_ok, count + 1)
                for t in range(NT):
                    last = nc.vector.tensor_scalar(dst[:, t, :], res[:, t, :], mv[:, t, 0:1], rstd[:, 1, t:t + 1],
                                                   ALU.subtract, ALU.mult)
                last.then_inc(done, 1)

            for s, it in program():
                what = it[0]
                if what == "s":
                    mm = it[1]
                    m = BT * max(s, 0) + mm
                    c, qt = (m % GT) // NT, m % NT
                    g = m // GT
                    if m % GT == 0:
                        wait(dve, m_parts, g - 1)
                    dve.wait_ge(ps_s, m + 1)
                    nc.vector.tensor_reduce(negmax[:, g % 2, qt, c:c + 1], s_bank[m % 2][:, :], AX.X,
                                            ALU.max, negate=True).then_inc(ev_s, 1)
                elif what == "qk":
                    b, i = s + 1, it[1]
                    n = 2 * b + i
                    pt = parts[i]
                    A, Bs, C = ((0, 1, 2), (3, 4), 5) if i == 0 else ((0, 3, 5), (1, 4), 2)
                    dve.wait_ge(ev_qk, n + 1)
                    if b:
                        for j in range(NG):
                            dve.wait_ge(rep[j], 16 * 2 * GH * b)
                    nc.vector.tensor_copy(pt[:, A[0], :], qk_f[i][:, :]).then_inc(qk_step, 1)
                    dve.wait_ge(qk_step, 3 * n + 1)
                    nc.vector.tensor_tensor(qk_r[i][:, :], qk_f[i][:, :], pt[:, A[0], :], ALU.subtract).then_inc(qk_step, 1)
                    for a in A[1:]:
                        nc.vector.tensor_copy(pt[:, a, :], pt[:, A[0], :])
                    dve.wait_ge(qk_step, 3 * n + 2)
                    nc.vector.tensor_copy(pt[:, Bs[0], :], qk_r[i][:, :]).then_inc(qk_step, 1)
                    dve.wait_ge(qk_step, 3 * n + 3)
                    nc.vector.tensor_copy(pt[:, Bs[1], :], pt[:, Bs[0], :])
                    nc.vector.tensor_tensor(pt[:, C, :], qk_r[i][:, :], pt[:, Bs[0], :], ALU.subtract).then_inc(qk_parts, 1)
                elif what == "v":
                    b = max(s, 0)
                    dve.wait_ge(ps_v, b + 1)
                    if b == 0:
                        dve.wait_ge(vzero, 2)
                    wait(dve, ps_pv, NG * NT * b)
                    nc.vector.tensor_tensor(v_sb[:, :, :, 0:HD].rearrange("p t h d -> p (t h) d"),
                                            f_bank[0][:, :].rearrange("p (a d) -> p a d", d=HD),
                                            vb[:, :, :].rearrange("p t (h d) -> p (t h) d", d=HD), ALU.add).then_inc(ev_v, 1)
                elif what == "oT":
                    g = NG * s + it[1]
                    j = g % NG
                    dve.wait_ge(ps_oT, g + 1)
                    sums = t_bank[:, :].rearrange("p (a w) -> p a w", w=VW)
                    nc.vector.reciprocal(rden[:, :], sums[:, :, HD]).then_inc(rd_oT, 1)
                    dve.wait_ge(rd_oT, g + 1)
                    if j == 0:
                        wait(dve, ps_aT, g // NG)
                    for t in range(NT):
                        last = nc.vector.tensor_tensor(
                            attn[:, t, GH * HD * j:GH * HD * (j + 1)].rearrange("p (c d) -> p c d", d=HD),
                            sums[:, GH * t:GH * (t + 1), 0:HD],
                            rden[:, GH * t:GH * (t + 1)].unsqueeze(2).broadcast_to([P, GH, HD]), ALU.mult)
                    last.then_inc(ev_oT, 1)
                elif what == "fc":
                    dve.wait_ge(ps_fc, s)
                    dve.wait_ge(resb, s)
                    nc.vector.tensor_tensor(res[:, :, :].rearrange("p t c -> p (t c)"), f_bank[1][:, :],
                                            x_res[:, :, :].rearrange("p t c -> p (t c)"), ALU.add).then_inc(ln_step, 1)
                    layernorm(2 * (s - 1), x1, x1_ok)
                elif what == "x1T":
                    dve.wait_ge(ps_x1T, s)
                    wait(dve, ps_w2, NK * (s - 1))
                    nc.vector.tensor_copy(x1T[0][:, :], t_bank[:, :]).then_inc(hi_x1T, 1)
                    dve.wait_ge(hi_x1T, s)
                    nc.vector.tensor_tensor(x1T[1][:, :], t_bank[:, :], x1T[0][:, :].bitcast(F32), ALU.subtract).then_inc(ev_x1T, 1)
                elif what == "w12":
                    k = it[1]
                    n = NK * (s - 1) + k
                    dve.wait_ge(ps_w2, n + 1)
                    dve.wait_ge(ev_w1, n + 1)
                    wait(dve, lo0, n - 1)
                    nc.vector.scalar_tensor_tensor(hf[:, k % 2, :], f_bank[1][:, :], hs[:, 1, k:k + 1], silu[:, k % 2, :],
                                                   ALU.mult, ALU.mult).then_inc(ev_w2, 1)
                    dve.wait_ge(ev_w2, n + 1)
                    if k == 0:
                        wait(dve, ps_w3, s - 1)
                    nc.vector.tensor_copy(act0[0][:, k, :], hf[:, k % 2, :]).then_inc(hi0, 1)
                elif what == "h":
                    layer, k = it[1], it[2]
                    n = NK * (2 * (s - 1) + layer) + k
                    dve.wait_ge(ev_h, n + 1)
                    if k == 0 and layer == 0:
                        wait(dve, ps_h, 2 * NK * (s - 1))
                    elif k == 0:
                        wait(dve, ps_h, NK * (2 * (s - 1) + 1))
                    nc.vector.tensor_copy((act1, act2)[layer][0][:, k, :], gf[:, k % 2, :]).then_inc(hi_g, 1)
                elif what == "w3":
                    dve.wait_ge(ps_w3, s)
                    nc.vector.tensor_tensor(res[:, :, :].rearrange("p t c -> p (t c)"), f_bank[0][:, :],
                                            s3[:, :, :].rearrange("p t c -> p (t c)"), ALU.mult).then_inc(ev_w3, 1)
                    dve.wait_ge(ev_w3, s)
                    nc.vector.tensor_tensor(res[:, :, :], res[:, :, :], x1[:, :, :], ALU.add).then_inc(ln_step, 1)
                    wait(dve, st_out, 16 * (s - 1))
                    layernorm(2 * (s - 1) + 1, y, y_ok)
                elif what == "wt":
                    u = it[1]
                    dve.wait_ge(hi_wt, u + 1)
                    nc.vector.tensor_tensor(wt_dst(u, 1), f_bank[u % 2][:, :], wt_dst(u, 0).bitcast(F32), ALU.subtract).then_inc(ev_wt, 1)

        @block.gpsimd
        def _(pool):
            nc.gpsimd.memset(ident[:, :], 0.0).then_inc(ids, 1)
            nc.gpsimd.memset(ident16[:, :], 0.0).then_inc(ids, 1)
            pool.wait_ge(ids, 2)
            for m in (ident, ident16):
                nc.gpsimd.affine_select(out=m[:, :], in_=m[:, :], compare_op=ALU.not_equal, fill=1.0, base=0,
                                        pattern=[[-1, P]], channel_multiplier=1).then_inc(ids, 1)
            pool.wait_ge(ids, 4)
            q_rows = stack[0][:, :, :].rearrange("p h n -> p (h n)").bitcast(F32)
            nc.gpsimd.memset(q_rows[32:64, :], 0.0).then_inc(zeros, 1)
            pool.wait_ge(zeros, 1)
            nc.gpsimd.memset(q_rows[64:P, :], 0.0).then_inc(zeros, 1)
            pool.wait_ge(zeros, 2)
            nc.gpsimd.memset(v_sb[:, :, :, :], 0.0).then_inc(vzero, 1)
            pool.wait_ge(vzero, 1)
            nc.gpsimd.memset(v_sb[:, :, :, HD:HD + 1], 1.0).then_inc(vzero, 1)

            nc.gpsimd.memset(mhalf[:, :], -0.5).then_inc(vzero, 1)

            def inv_sqrt(count):
                pool.wait_ge(ln_step, 4 * count + 4)
                if count == 0:
                    pool.wait_ge(vzero, 3)
                nc.gpsimd.tensor_tensor(rstd[:, 1, :], rstd[:, 0, :], mhalf[:, :], ALU.pow).then_inc(rs_ok, 1)

            for s, it in program():
                what = it[0]
                if what == "fc":
                    inv_sqrt(2 * (s - 1))
                elif what == "w3":
                    inv_sqrt(2 * (s - 1) + 1)
                if what == "mT":
                    g = NG * s + it[1] if s >= 0 else 0
                    pool.wait_ge(ev_s, GT * (g + 1))
                    wait(pool, ps_mT, g)
                    nm = negmax[:, g % 2]
                    nc.gpsimd.tensor_copy(mparts[:, :, 0, :], nm).then_inc(m_step, 1)
                    pool.wait_ge(m_step, 3 * g + 1)
                    nc.gpsimd.tensor_tensor(mres[:, :, :], nm, mparts[:, :, 0, :], ALU.subtract).then_inc(m_step, 1)
                    pool.wait_ge(m_step, 3 * g + 2)
                    nc.gpsimd.tensor_copy(mparts[:, :, 1, :], mres[:, :, :]).then_inc(m_step, 1)
                    pool.wait_ge(m_step, 3 * g + 3)
                    nc.gpsimd.tensor_tensor(mparts[:, :, 2, :], mres[:, :, :], mparts[:, :, 1, :],
                                            ALU.subtract).then_inc(m_parts, 1)
                elif what == "pv" and it[1] == 1 and it[2] == 0 and s < B:
                    if s == 0:
                        pool.wait_ge(ld_bias, 16 * (2 + 2 * NT))
                    pool.wait_ge(ld_res, 16 * (s + 1))
                    nc.gpsimd.tensor_tensor(x_res[:, :, :], x_res[:, :, :], x_res[:, :, :], ALU.add).then_inc(res2, 1)
                    pool.wait_ge(res2, s + 1)
                    nc.gpsimd.tensor_tensor(x_res[:, :, :], x_res[:, :, :], fcb[:, :, :], ALU.add).then_inc(resb, 1)
                elif what == "w12":
                    k = it[1]
                    n = NK * (s - 1) + k
                    pool.wait_ge(hi0, n + 1)
                    nc.gpsimd.tensor_tensor(act0[1][:, k, :], hf[:, k % 2, :], act0[0][:, k, :].bitcast(F32),
                                            ALU.subtract).then_inc(lo0, 1)
                elif what == "h":
                    layer, k = it[1], it[2]
                    n = NK * (2 * (s - 1) + layer) + k
                    pool.wait_ge(hi_g, n + 1)
                    a = (act1, act2)[layer]
                    nc.gpsimd.tensor_tensor(a[1][:, k, :], gf[:, k % 2, :], a[0][:, k, :].bitcast(F32),
                                            ALU.subtract).then_inc(lo_g, 1)


_INS = ['L0_attn_x', 'L0_attn_qkv_w', 'L0_attn_qkv_b', 'L0_attn_fc_w', 'L0_attn_fc_b', 'L0_ffn_w1_w', 'L0_ffn_w1_s',
        'L0_ffn_w2_w', 'L0_ffn_w2_s', 'L0_ffn_h1_w', 'L0_ffn_h1_s', 'L0_ffn_h2_w', 'L0_ffn_h2_s', 'L0_ffn_w3_w',
        'L0_ffn_w3_s']
_OUTS = [((4, 512, 128), 'float32')]


def kernel(**inputs):
    import numpy as _np
    import concourse.bacc as _bacc
    from concourse import mybir as _mybir
    from concourse.bass_utils import run_bass_kernel_spmd as _run

    nc = _bacc.Bacc("TRN2", target_bir_lowering=False, num_devices=1)
    arrays, args = {}, []
    for name in _INS:
        a = _np.ascontiguousarray(inputs[name])
        arrays[f"in_{name}_dram"] = a
        args.append(nc.dram_tensor(f"in_{name}_dram", a.shape, _mybir.dt.from_np(a.dtype), kind="ExternalInput").ap())
    for i, (shape, dtype) in enumerate(_OUTS):
        dt = _mybir.dt.from_np(_np.dtype(dtype))
        args.append(nc.dram_tensor(f"out_{i}_dram", shape, dt, kind="ExternalOutput").ap())
    post_ln_block_kernel(nc, *args)
    r = _run(nc, [arrays], core_ids=[0])
    got = tuple(r.results[0][f"out_{i}_dram"] for i in range(len(_OUTS)))
    return got[0]
```

```python
import numpy as np

import concourse.bass as bass
from concourse import mybir
from contextlib import ExitStack


def post_ln_block_kernel(
    nc: bass.Bass,
    x: bass.AP,
    qkv_w: bass.AP,
    qkv_b: bass.AP,
    fc_w: bass.AP,
    fc_b: bass.AP,
    w1_w: bass.AP,
    w1_s: bass.AP,
    w2_w: bass.AP,
    w2_s: bass.AP,
    h1_w: bass.AP,
    h1_s: bass.AP,
    h2_w: bass.AP,
    h2_s: bass.AP,
    w3_w: bass.AP,
    w3_s: bass.AP,
    out: bass.AP,
):
    F32, F32R, BF16 = mybir.dt.float32, mybir.dt.float32r, mybir.dt.bfloat16
    ALU = mybir.AluOpType
    ACT = mybir.ActivationFunctionType
    AX = mybir.AxisListType

    P = 128
    B, N, D = x.shape
    H = 16
    HD = D // H
    HID = w1_w.shape[0]
    SCALE = float(HD) ** -0.5
    EPS = 1e-5
    NT = N // P
    NK = HID // P
    GH = 4
    NG = H // GH
    GT = GH * NT
    BT = NG * GT
    NPART = 3
    SLOTS = 6
    SR = SLOTS * HD
    MROW = 96
    VW = 32
    LEAD = 26
    TWO_ONES = float(np.array([0x3F803F80], np.uint32).view(np.float32)[0])
    WT = 3 + 2 * NK
    NP = 8
    assert D == P and HID == 512 and N == 512 and H == 16

    with ExitStack() as ctx:
        def sb(name, shape, dt):
            return ctx.enter_context(nc.sbuf_tensor(name, shape, dt))

        def sem(name):
            return ctx.enter_context(nc.semaphore(name))

        def bank(name):
            return ctx.enter_context(nc.psum_tensor(name, [P, 512], F32))

        s_bank = [bank(f"s_bank{i}") for i in range(2)]
        st_bank = [bank(f"st_bank{i}") for i in range(2)]
        pv_bank = bank("pv_bank")
        t_bank = bank("t_bank")
        f_bank = [bank(f"f_bank{i}") for i in range(2)]
        t_bank16 = t_bank[:, :].bitcast(BF16)

        ident = sb("ident", [P, P], F32)
        ident16 = sb("ident16", [P, P], BF16)
        h1_nat = sb("h1_nat", [P, NK, HID], F32)
        work = sb("work", [P, 6, N], F32)
        y = sb("y", [P, NT, D], F32)
        res = sb("res", [P, NT, D], F32)
        qkv_nat, fc_nat = res[:, 0:3, :], res[:, 3, :]
        h_nat = [h1_nat[:, :, :], work[:, 0:4, :]]
        w_nat = work[:, 4:6, :].rearrange("p w (t c) -> p w t c", t=NK)
        w3_nat = y[:, :, :].rearrange("p t c -> p (t c)")
        qkvT = sb("qkvT", [P, 3, D], F32)
        fcT = sb("fcT", [P, D], F32)
        w12T = [sb(f"w12T{i}", [P, 2, HID], F32R) for i in range(2)]
        hT = [sb(f"hT{i}", [P, 2 * NK, HID], F32R) for i in range(2)]
        w3T = [sb(f"w3T{i}", [P, NK, D], F32R) for i in range(2)]
        qkb = sb("qkb", [P, 2], F32)
        vb = sb("vb", [P, NT, D], F32)
        fcb = sb("fcb", [P, NT, D], F32)
        s3 = sb("s3", [P, NT, D], F32)
        hs = sb("hs", [P, 4, NK], F32)

        x_in = sb("x_in", [P, NT, D], F32)
        x_res = sb("x_res", [P, NT, D], F32)
        xT = sb("xT", [P, N], F32)
        qk_f = [sb(f"qk_f{i}", [P, N], F32) for i in range(2)]
        qk_r = [sb(f"qk_r{i}", [P, N], F32) for i in range(2)]
        parts = [sb(f"parts{i}", [P, SLOTS, N], BF16) for i in range(2)]
        stack = [sb(f"stack{i}", [P, H, N], BF16) for i in range(2)]
        v_sb = sb("v_sb", [P, NT, H, VW], F32)
        negmax = sb("negmax", [P, 2, NT, GH], F32)
        mres = sb("mres", [P, NT, GH], F32)
        mparts = sb("mparts", [P, NT, NPART, GH], BF16)
        mT = sb("mT", [GH * NPART, N], BF16)
        prob = sb("prob", [P, NP, N], F32)
        oT = sb("oT", [P, N], F32)
        rden = sb("rden", [P, NT * GH], F32)
        attn = sb("attn", [P, NT, D], F32)
        aT = sb("aT", [P, N], F32)
        warm = sb("warm", [P, 1], F32)
        stats = sb("stats", [P, NT, 6], F32)
        mv = sb("mv", [P, NT, 2], F32)
        rstd = sb("rstd", [P, 2, NT], F32)
        mhalf = sb("mhalf", [P, NT], F32)
        wlow = sb("wlow", [P, WT], F32)
        wlow1 = sb("wlow1", [P, 1], F32)
        wflag = sb("wflag", [1, 1], F32)
        x1 = sb("x1", [P, NT, D], F32)
        x1T = [sb(f"x1T{i}", [P, N], F32R) for i in range(2)]
        silu, hf, gf = work[:, 0:2, :], work[:, 2:4, :], work[:, 4:6, :]
        act0 = [sb(f"act0_{i}", [P, NK, N], F32R) for i in range(2)]
        act1 = [sb(f"act1_{i}", [P, NK, N], F32R) for i in range(2)]
        act2 = act0

        ld_qkv, ld_qkb, ld_vb, ld_fcb, ld_x, ld_res, ld_w, ld_h, ld_w3, ld_s = (
            sem(n) for n in ("ld_qkv", "ld_qkb", "ld_vb", "ld_fcb", "ld_x", "ld_res", "ld_w", "ld_h", "ld_w3", "ld_s"))
        st_out = sem("st_out")
        ids, ones, zeros, vzero = sem("ids"), sem("ones"), sem("zeros"), sem("vzero")
        ps_wq, ev_wq = sem("ps_wq"), sem("ev_wq")
        ps_wt, hi_wt, ev_wt = sem("ps_wt"), sem("hi_wt"), sem("ev_wt")
        ps_xT, ev_xT = sem("ps_xT"), sem("ev_xT")
        ps_qk, ev_qk = sem("ps_qk"), sem("ev_qk")
        qk_step, qk_parts = ([sem(f"{n}{i}") for i in range(2)] for n in ("qk_step", "qk_parts"))
        ps_v, ev_v = sem("ps_v"), sem("ev_v")
        rep = [sem(f"rep{h}") for h in range(H)]
        ps_s, ev_s = sem("ps_s"), sem("ev_s")
        m_step, m_parts, ps_mT, ev_mT = (sem(n) for n in ("m_step", "m_parts", "ps_mT", "ev_mT"))
        mrow = [sem(f"mrow{j}") for j in range(NG)]
        ps_st, ev_st, ps_pv = sem("ps_st"), sem("ev_st"), sem("ps_pv")
        ev_pv, ps_oT, rd_oT, ev_oT = (sem(n) for n in ("ev_pv", "ps_oT", "rd_oT", "ev_oT"))
        ps_aT, ev_aT, ps_fc = (sem(n) for n in ("ps_aT", "ev_aT", "ps_fc"))
        lo_max, ps_low, low_ok = sem("lo_max"), sem("ps_low"), sem("low_ok")
        res2, resb = sem("res2"), sem("resb")
        rs_ok = sem("rs_ok")
        ln_step, x1_ok, y_ok = sem("ln_step"), sem("x1_ok"), sem("y_ok")
        ps_x1T, hi_x1T, ev_x1T = sem("ps_x1T"), sem("hi_x1T"), sem("ev_x1T")
        ps_w1, ps_w2, ev_w1, ev_w2 = (sem(n) for n in ("ps_w1", "ps_w2", "ev_w1", "ev_w2"))
        hi0, lo0 = sem("hi0"), sem("lo0")
        ps_h, ev_h, hi_g, lo_g = (sem(n) for n in ("ps_h", "ev_h", "hi_g", "lo_g"))
        ps_w3, ev_w3 = sem("ps_w3"), sem("ev_w3")

        def wait(eng, s, value):
            if not isinstance(value, int) or value > 0:
                eng.wait_ge(s, value)

        LN_STEPS = 5

        def order(s):
            now, nxt, prev = s < B, s + 1 < B, s >= 1
            at = {}

            def put(j, i, cost, *item):
                at.setdefault((j, i), []).append((cost, item))

            for j in range(NG if now else 1):
                if j or prev:
                    put(j, 3, 0.9, "pv", j - 1, 3)
                    put(j, 5, 0, "oT_in", j - 1)
                    put(j, 7, 0.44, "oT", j - 1)
                    put(j, 8, 0, "oT_rec", j - 1)
                    put(j, 9, 0, "oT_mul", j - 1)
                if now:
                    for k in range(NT - 1):
                        put(j, 7 + 4 * k, 0.9, "pv", j, k)
                    if j < NG - 1 or nxt:
                        put(j, 8, 0, "m_split", j + 1)
                        put(j, 11, 0.22, "mT", j + 1)
                        put(j, 12, 0, "mT_in", j + 1)
            if prev:
                if now:
                    put(0, 2, 0.9, "v")
                    put(0, 4, 0, "v_in")
                put(0, 13, 0.44, "aT")
                put(0, 14, 0, "aT_in")
                put(0, 15, 0.9, "fc")
                for k in range(LN_STEPS):
                    put(1, (0, 1, 2, 3, 5)[k], 0, "ln", k, 2 * (s - 1))
                put(1, 13, 0.44, "x1T")
                put(1, 14, 0, "x1T_hi")
                put(1, 15, 0, "x1T_lo")
                if now:
                    for k in range(NK):
                        put(2, 1, 1.2, "w12", k)
                        if k:
                            put(2, 1, 0, "w12_hi", k - 1)
                    put(2, 1, 0, "w12_hi", NK - 1)
                else:
                    for k in range(NK):
                        put(2, 1, 0, "w12", k)
                        if k:
                            put(2, 1, 0, "w12_lo", k - 1)
                        put(2, 1, 0, "w12_hi", k)
                    put(2, 1, 0, "w12_lo", NK - 1)
                for layer in range(2):
                    j, i = ((2, 9), (3, 1))[layer]
                    if not now:
                        put(j, i, 0, "layer", layer)
                    for k in range(NK):
                        put(j, i, 1.73, "h", layer, k)
                put(3, 11, 2.5, "w3")
                put(3, 13, 0, "w3_in")
                put(3, 14, 0, "ln", 0, 2 * (s - 1) + 1)
                put(3, 15, 0, "ln", 1, 2 * (s - 1) + 1)
                if not now:
                    for k in range(2, LN_STEPS):
                        put(3, 15, 0, "ln", k, 2 * (s - 1) + 1)
            if s >= 2:
                for k in range(2, LN_STEPS):
                    put(0, (0, 1, 3)[k - 2], 0, "ln", k, 2 * (s - 2) + 1)
            if nxt:
                put(0, 4, 0.44, "xT")
                put(0, 5, 0, "xT_in")
                put(0, 6, 0.9, "qk", 0)
                put(0, 6, 0.9, "qk", 1)
                put(0, 7, 0, "qk_in", 0)
                put(0, 8, 0, "qk_in", 1)
                for k in range(4):
                    for i in range(2):
                        put(0, 10 + (0, 0, 1, 2, 3, 3, 4, 5)[2 * k + i], 0, "split", k, i)
                put(1, 0, 0, "spread", 0)
                put(2, 0, 0, "spread", 1)
                put(3, 0, 0, "spread", 2)
            if s == 0:
                for u in range(WT):
                    j, i = 1 + u // 4, 1 + 3 * (u % 4)
                    put(j, i, 0.44, "wt", u)
                    put(j, i + 1, 0, "wt_hi", u)
                    put(j, i + 2, 0, "wt_lo", u)
                put(3, 12, 0.1, "w_low")
            if prev and now:
                put(0, 3, 0, "spread", NG - 1)

            items = []
            for j in range(NG):
                for i in range(GT):
                    if now:
                        items.append((0.22, ("st", j, i)))
                    items += at.get((j, i), [])
            if not now:
                return [it for _, it in items]
            first, tiles = LEAD, BT
            total = sum(c for c, _ in items)
            placed, t, r = [], 0.0, 0
            for c, it in items:
                while r < tiles and t >= total * r / tiles:
                    if s * BT + first + r < B * BT:
                        placed.append(("s", first + r))
                    r += 1
                if it[0] == "m_split":
                    while first + r < (it[1] + 1) * GT and r < tiles:
                        placed.append(("s", first + r))
                        r += 1
                placed.append(it)
                t += c
            while r < tiles and s * BT + first + r < B * BT:
                placed.append(("s", first + r))
                r += 1
            return placed

        def prologue():
            return ([("xT",), ("xT_in",), ("qk", 0), ("qk", 1), ("qk_in", 0), ("qk_in", 1)]
                    + [("split", k, i) for i in range(2) for k in range(4)] + [("spread", j) for j in range(2)]
                    + [("v",)] + [("s", m) for m in range(GT)] + [("m_split", 0)] + [("s", m) for m in range(GT, GT + 4)]
                    + [("mT", 0), ("mT_in", 0)] + [("s", m) for m in range(GT + 4, LEAD)] + [("v_in",)]
                    + [("spread", j) for j in range(2, NG)])

        def program(slots):
            for s in slots:
                for it in (order(s) if s >= 0 else prologue()):
                    yield s, it

        ALL = range(-1, B + 1)

        last_banks = [s_bank + st_bank, f_bank + [pv_bank, t_bank]]

        def w1_bank(s, k):
            return last_banks[0][k] if s == B else f_bank[0]

        def w2_bank(s, k):
            return last_banks[1][k] if s == B else f_bank[1]

        def h_bank(s, layer, k):
            return last_banks[layer][k] if s == B else f_bank[k % 2]

        block = ctx.enter_context(nc.Block())

        @block.sync
        def _(sp):
            sp.dma_start(x_in[:, :, :], x[0].rearrange("(t p) c -> p t c", p=P)).then_inc(ld_x, 16)
            sp.dma_start(qkv_nat, qkv_w.rearrange("(t p) c -> p t c", p=P)).then_inc(ld_qkv, 16)
            sp.dma_start(fc_nat, fc_w).then_inc(ld_qkv, 16)
            qkv_bh = qkv_b.rearrange("(h k d) -> k h d", k=3, d=HD)
            for i in range(2):
                sp.dma_start(qkb[:, i:i + 1], qkv_bh[i]).then_inc(ld_qkb, 16)

            def more_loads():
                for i, w in enumerate((w1_w, w2_w)):
                    sp.dma_start(w_nat[:, i, :, :], w.rearrange("(t p) c -> p t c", p=P)).then_inc(ld_w, 16)
                for i, w in enumerate((h1_w, h2_w)):
                    sp.dma_start(h_nat[i], w.rearrange("(t p) c -> p t c", p=P)).then_inc(ld_h, 16)
                sp.dma_start(w3_nat, w3_w).then_inc(ld_w3, 16)
                sp.dma_start(x_res[:, :, :], x[0].rearrange("(t p) c -> p t c", p=P)).then_inc(ld_res, 16)
                for t in range(NT):
                    sp.dma_start(fcb[:, t, :], fc_b.partition_broadcast(P)).then_inc(ld_fcb, 16)
                    sp.dma_start(s3[:, t, :], w3_s.partition_broadcast(P)).then_inc(ld_s, 16)
                for i, w in enumerate((w1_s, w2_s, h1_s, h2_s)):
                    sp.dma_start(hs[:, i, :], w.rearrange("(k p) -> p k", p=P),
                                 allow_slow_non_contiguous=True).then_inc(ld_s, 16)

            for t in range(NT):
                sp.dma_start(vb[:, t, :].rearrange("p (h d) -> p h d", d=HD),
                             qkv_bh[2].partition_broadcast(P)).then_inc(ld_vb, 16)

            def spread(b, j):
                if b == 0:
                    wait(sp, ones, 2 * (j + 1))
                    wait(sp, zeros, 2 * (j + 1))
                wait(sp, ps_st, BT * (b - 1) + GT * (j + 1))
                for i in range(2):
                    wait(sp, qk_parts[i], b + 1)
                    for h in range(GH * j, GH * (j + 1)):
                        sp.dma_start(stack[i][0:SR, h, :],
                                     parts[i][HD * h:HD * h + HD, :, :]).then_inc(rep[h], 16)

            for s, it in program(ALL):
                if it[0] == "xT_in" and s + 2 < B:
                    wait(sp, ps_xT, s + 2)
                    sp.dma_start(x_in[:, :, :], x[s + 2].rearrange("(t p) c -> p t c", p=P)).then_inc(ld_x, 16)
                elif it[0] == "spread":
                    j = it[1]
                    spread(s if s >= 0 and j == NG - 1 else s + 1, j)
                elif it[0] == "mT_in":
                    g = NG * s + it[1] if s >= 0 else 0
                    wait(sp, ev_mT, g + 1)
                    j = it[1] % NG
                    sp.dma_start(stack[0][MROW:MROW + NPART, GH * j:GH * (j + 1), :], mT[:, :]).then_inc(mrow[j], 16)
                    if s == -1:
                        more_loads()
                elif it[0] == "ln" and it[1] == 2 and it[2] % 2 == 0 and s < B:
                    wait(sp, ln_step, 8 * (s - 1) + 1)
                    sp.dma_start(x_res[:, :, :], x[s].rearrange("(t p) c -> p t c", p=P)).then_inc(ld_res, 16)
                elif it[0] == "ln" and it[1] == 4 and it[2] % 2 == 1:
                    b = it[2] // 2
                    wait(sp, y_ok, b + 1)
                    sp.dma_start(out[b].rearrange("(t p) c -> p t c", p=P), y[:, :, :]).then_inc(st_out, 16)
            sp.wait_ge(st_out, 16 * B)

        @block.tensor
        def _(pe):
            def transpose4(dst, src):
                for t in range(4):
                    last = nc.tensor.transpose(dst[:, t * P:(t + 1) * P], src(t), ident[:, :])
                return last

            pe.wait_ge(ids, 4)
            pe.wait_ge(ld_qkv, 32)
            for t in range(3):
                nc.tensor.transpose(f_bank[0][:, t * P:(t + 1) * P], qkv_nat[:, t, :], ident[:, :])
            nc.tensor.transpose(f_bank[0][:, 3 * P:4 * P], fc_nat, ident[:, :]).then_inc(ps_wq, 1)

            def scores_q(m, b):
                j, c, qt = m // GT, (m % GT) // NT, m % NT
                h = GH * j + c
                if qt == 0:
                    wait(pe, rep[h], 16 * 2 * (b + 1))
                wait(pe, ev_s, b * BT + m - 1)
                nc.tensor.matmul(s_bank[m % 2][:, :], stack[0][0:MROW, h, qt * P:(qt + 1) * P],
                                 stack[1][0:MROW, h, :], start=True, stop=True).then_inc(ps_s, 1)

            def scores_k(n, b):
                j, kt, c = n // GT, (n % GT) // GH, n % GH
                h = GH * j + c
                if n % GT == 0:
                    wait(pe, mrow[j], 16 * (b + 1))
                wait(pe, ev_st, b * BT + n - 1)
                nc.tensor.matmul(st_bank[n % 2][:, :], stack[1][:, h, kt * P:(kt + 1) * P], stack[0][:, h, :], start=True, stop=True).then_inc(ps_st, 1)

            def pv(g, kt):
                wait(pe, ev_st, (NT * g + kt + 1) * GH)
                if kt == 0:
                    wait(pe, ev_pv, g)
                    wait(pe, ev_v, g // NG + 1)
                j = g % NG
                for c in range(GH):
                    last = nc.tensor.matmul(pv_bank[VW * c:VW * c + VW, :], v_sb[:, kt, GH * j + c, :],
                                            prob[:, (GH * kt + c) % NP, :], start=kt == 0, stop=kt == NT - 1)
                last.then_inc(ps_pv, 1)

            def split_mm(dst, lefts, rights, first, last):
                pairs = [(w, v) for w in lefts for v in rights]
                for n, (w, v) in enumerate(pairs):
                    mm = nc.tensor.matmul(dst, w, v, start=first and n == 0, stop=last and n == len(pairs) - 1)
                return mm

            def step(s, it, wparts):
                what = it[0]
                if what == "s":
                    m = it[1]
                    scores_q(m % BT, max(s, 0) + m // BT)
                elif what == "st":
                    scores_k(GT * it[1] + it[2], s)
                elif what == "pv":
                    pv(NG * s + it[1], it[2])
                elif what == "xT":
                    b = s + 1
                    wait(pe, ld_x, 16 * (b + 1))
                    if s >= 0:
                        wait(pe, ev_mT, NG * s + 1)
                    transpose4(t_bank, lambda t: x_in[:, t, :]).then_inc(ps_xT, 1)
                elif what == "qk":
                    b, i = s + 1, it[1]
                    wait(pe, ev_xT, b + 1)
                    if s == -1:
                        wait(pe, ev_wq, 4)
                    elif i == 0:
                        wait(pe, ev_v, s + 1)
                    elif s == 0:
                        wait(pe, ev_qk, 2)
                    else:
                        wait(pe, ev_h, 2 * NK * (s - 1))
                    nc.tensor.matmul(f_bank[i][:, :], qkvT[:, i, :], xT[:, :], start=True, stop=True).then_inc(ps_qk, 1)
                elif what == "v":
                    b = max(s, 0)
                    wait(pe, ev_xT, b + 1)
                    if s >= 2:
                        wait(pe, ev_w3, s - 1)
                    elif s == 1:
                        wait(pe, ev_wt, WT)
                    else:
                        wait(pe, ev_qk, 1)
                    for t in range(NT):
                        last = nc.tensor.matmul(f_bank[0][:, t * P:(t + 1) * P], xT[:, t * P:(t + 1) * P],
                                                qkvT[:, 2, :], start=True, stop=True)
                    last.then_inc(ps_v, 1)
                elif what == "mT":
                    g = NG * s + it[1] if s >= 0 else 0
                    wait(pe, m_parts, g + 1)
                    if g < 2:
                        wait(pe, ev_xT, g + 1)
                    else:
                        wait(pe, ev_oT, g - 1)
                    for t in range(NT):
                        last = nc.tensor.transpose(t_bank16[0:GH * NPART, t * P:(t + 1) * P],
                                                   mparts[:, t, :, :].rearrange("p m c -> p (m c)"), ident16[:, :])
                    last.then_inc(ps_mT, 1)
                elif what == "oT":
                    g = NG * s + it[1]
                    wait(pe, ev_pv, g + 1)
                    j = it[1]
                    if j == -1 and s + 1 < B:
                        wait(pe, ev_xT, s + 2)
                    elif j == -1 and s < B:
                        wait(pe, ev_mT, g + 2)
                    elif j == -1:
                        wait(pe, ev_oT, g)
                    elif j == 0 and s >= 1:
                        wait(pe, ev_aT, s)
                    elif j == 1 and s >= 1:
                        wait(pe, ev_x1T, s)
                    else:
                        wait(pe, ev_mT, g + 2)
                    transpose4(t_bank, lambda t: oT[:, t * P:(t + 1) * P]).then_inc(ps_oT, 1)
                elif what == "aT":
                    wait(pe, ev_oT, NG * s)
                    if s < B:
                        wait(pe, ev_mT, NG * s + 2)
                    transpose4(t_bank, lambda t: attn[:, t, :]).then_inc(ps_aT, 1)
                elif what == "fc":
                    wait(pe, ev_aT, s)
                    if s + 1 < B:
                        wait(pe, ev_qk, 2 * (s + 2))
                    else:
                        wait(pe, ev_h, 2 * NK * (s - 1))
                    for t in range(NT):
                        last = nc.tensor.matmul(f_bank[1][:, t * P:(t + 1) * P], aT[:, t * P:(t + 1) * P],
                                                fcT[:, :], start=True, stop=True)
                    last.then_inc(ps_fc, 1)
                elif what == "x1T":
                    wait(pe, x1_ok, s)
                    if s < B:
                        wait(pe, ev_mT, NG * s + 3)
                    else:
                        wait(pe, ev_aT, s)
                    transpose4(t_bank, lambda t: x1[:, t, :]).then_inc(ps_x1T, 1)
                elif what == "w12":
                    k = it[1]
                    cols = slice(k * P, (k + 1) * P)
                    if k == 0:
                        wait(pe, ev_x1T, s)
                        wait(pe, ev_wt, WT)
                        wait(pe, ln_step, 8 * (s - 1) + 1)
                        if s + 1 < B:
                            wait(pe, ev_qk, 2 * (s + 2))
                        elif s < B:
                            wait(pe, ev_v, s + 1)
                        else:
                            wait(pe, ev_w3, s - 1)
                    elif s < B:
                        wait(pe, ev_w1, NK * (s - 1) + k)
                    if s == B and k == 0:
                        wait(pe, ev_s, B * BT)
                        wait(pe, ev_st, B * BT)
                        wait(pe, ev_pv, B * NG)
                    xs = [x1T[0][:, :], x1T[1][:, :]]
                    split_mm(w1_bank(s, k)[:, :], [w[:, 0, cols] for w in w12T[:wparts]], xs, True, True).then_inc(ps_w1, 1)
                    if k and s < B:
                        wait(pe, ev_w2, NK * (s - 1) + k)
                    split_mm(w2_bank(s, k)[:, :], [w[:, 1, cols] for w in w12T[:wparts]], xs, True, True).then_inc(ps_w2, 1)
                elif what == "layer":
                    layer = it[1]
                    src = (act0, act1)[layer]
                    hi, lo = ((hi0, lo0), (hi_g, lo_g))[layer]
                    before = NK * (B - 1) if layer == 0 else NK * 2 * (B - 1)
                    wait(pe, (ev_w1, ev_w2)[layer], NK * B)
                    for kk in range(NK):
                        halves = [[0], [1]] if kk < NK - 1 else [[0, 1]]
                        for half in halves:
                            if 0 in half:
                                wait(pe, hi, before + kk + 1)
                            if 1 in half:
                                wait(pe, lo, before + kk + 1)
                            for k in range(NK):
                                last = split_mm(last_banks[layer][k][:, :],
                                                [w[:, NK * layer + kk, k * P:(k + 1) * P] for w in hT[:wparts]],
                                                [src[i][:, kk, :] for i in half],
                                                kk == 0 and 0 in half, kk == NK - 1)
                                if kk == NK - 1:
                                    last.then_inc(ps_h, 1)
                elif what == "h" and s < B:
                    layer, k = it[1], it[2]
                    cols = slice(k * P, (k + 1) * P)
                    done = NK * (2 * (s - 1) + layer)
                    src = (act0, act1)[layer]
                    if k == 0:
                        wait(pe, hi0 if layer == 0 else hi_g, (NK * s) if layer == 0 else done)
                        wait(pe, lo0 if layer == 0 else lo_g, (NK * s) if layer == 0 else done)
                    if layer == 0 and k < 2:
                        wait(pe, (ev_w1, ev_w2)[k], NK * s)
                    else:
                        wait(pe, ev_h, done + k - 1)
                    for kk in range(NK):
                        last = split_mm(f_bank[k % 2][:, :], [w[:, NK * layer + kk, cols] for w in hT[:wparts]],
                                        [a[:, kk, :] for a in src], kk == 0, kk == NK - 1)
                    last.then_inc(ps_h, 1)
                elif what == "w3" and s == B:
                    wait(pe, ev_h, NK * (2 * B - 1))
                    for kk in range(NK):
                        wait(pe, hi_g, 2 * NK * B - NK + kk + 1)
                        wait(pe, lo_g, 2 * NK * B - NK + kk + 1)
                        for t in range(NT):
                            last = split_mm(last_banks[0][t][:, 0:P], [a[:, kk, t * P:(t + 1) * P] for a in act2],
                                            [w[:, kk, :] for w in w3T[:wparts]], kk == 0, kk == NK - 1)
                    last.then_inc(ps_w3, 1)
                elif what == "w3":
                    wait(pe, hi_g, 2 * NK * s)
                    wait(pe, lo_g, 2 * NK * s)
                    wait(pe, ev_h, 2 * NK * s - 1)
                    for t in range(NT):
                        for kk in range(NK):
                            last = split_mm(f_bank[0][:, t * P:(t + 1) * P],
                                            [a[:, kk, t * P:(t + 1) * P] for a in act2],
                                            [w[:, kk, :] for w in w3T[:wparts]], kk == 0, kk == NK - 1)
                    last.then_inc(ps_w3, 1)
                elif what == "wt":
                    u = it[1]
                    if u == 0:
                        wait(pe, ev_qk, 4)
                    wait(pe, ev_wt, u - 1)
                    bank_ = f_bank[u % 2]
                    if u < 2:
                        wait(pe, ld_w, 32)
                        last = transpose4(bank_, lambda t: w_nat[:, u, t, :])
                    elif u < 2 + 2 * NK:
                        wait(pe, ld_h, 32)
                        layer, kk = (u - 2) // NK, (u - 2) % NK
                        last = transpose4(bank_, lambda t: h_nat[layer][:, t, kk * P:(kk + 1) * P])
                    else:
                        wait(pe, ld_w3, 16)
                        last = transpose4(bank_, lambda t: w3_nat[:, t * P:(t + 1) * P])
                    last.then_inc(ps_wt, 1)
                elif what == "w_low":
                    wait(pe, lo_max, 2)
                    nc.tensor.transpose(f_bank[1][0:1, 0:P], wlow1[:, :], ident[:, :]).then_inc(ps_low, 1)

            for s, it in program(range(-1, 1)):
                step(s, it, 2)
            pe.wait_ge(low_ok, 1)
            low = pe.value_load(wflag[:, :].bitcast(mybir.dt.int32))
            with pe.If(low == 0):
                for s, it in program(range(1, B + 1)):
                    step(s, it, 1)
            with pe.Else():
                for s, it in program(range(1, B + 1)):
                    step(s, it, 2)

        def wt_dst(u, part):
            if u < 2:
                return w12T[part][:, u, :]
            if u < 2 + 2 * NK:
                return hT[part][:, u - 2, :]
            return w3T[part][:, :, :].rearrange("p k c -> p (k c)")

        @block.scalar
        def _(act):
            act.wait_ge(ids, 4)
            nc.scalar.activation(warm[:, :], ident[:, 0:1], ACT.Exp)
            act.wait_ge(ld_qkb, 32)
            for s, it in program(ALL):
                what = it[0]
                if what == "st":
                    r = GT * it[1] + it[2]
                    n = BT * s + r
                    if n % GH == 0:
                        wait(act, ps_pv, n // GH - 1)
                    act.wait_ge(ps_st, n + 1)
                    nc.scalar.activation(prob[:, r % NP, :], st_bank[r % 2][:, :], ACT.Exp, scale=SCALE).then_inc(ev_st, 1)
                elif what == "xT_in":
                    act.wait_ge(ps_xT, s + 2)
                    if s >= 0:
                        act.wait_ge(ps_v, s + 1)
                    nc.scalar.activation(xT[:, :], t_bank[:, :], ACT.Copy).then_inc(ev_xT, 1)
                elif what == "qk_in":
                    b, i = s + 1, it[1]
                    act.wait_ge(ps_qk, 2 * b + i + 1)
                    wait(act, qk_parts[i], b)
                    nc.scalar.activation(qk_f[i][:, :], f_bank[i][:, :], ACT.Identity, bias=qkb[:, i:i + 1]).then_inc(ev_qk, 1)
                elif what == "mT_in":
                    g = NG * s + it[1] if s >= 0 else 0
                    act.wait_ge(ps_mT, g + 1)
                    if g:
                        act.wait_ge(mrow[(g - 1) % NG], 16 * ((g - 1) // NG + 1))
                    nc.scalar.activation(mT[:, :], t_bank16[0:GH * NPART, 0:N], ACT.Copy).then_inc(ev_mT, 1)
                elif what == "oT_in":
                    g = NG * s + it[1]
                    act.wait_ge(ps_pv, NT * (g + 1))
                    wait(act, ps_oT, g)
                    nc.scalar.activation(oT[:, :], pv_bank[:, :], ACT.Copy).then_inc(ev_pv, 1)
                elif what == "aT_in":
                    act.wait_ge(ps_aT, s)
                    wait(act, ps_fc, s - 1)
                    nc.scalar.activation(aT[:, :], t_bank[:, :], ACT.Copy).then_inc(ev_aT, 1)
                elif what == "w12":
                    k = it[1]
                    n = NK * (s - 1) + k
                    if n == 0:
                        act.wait_ge(ld_s, 16 * (NT + 4))
                    act.wait_ge(ps_w1, n + 1)
                    wait(act, ev_w2, n - 1)
                    nc.scalar.activation(silu[:, k % 2, :], w1_bank(s, k)[:, :], ACT.Silu, scale=hs[:, 0, k:k + 1]).then_inc(ev_w1, 1)
                elif what == "h":
                    layer, k = it[1], it[2]
                    n = NK * (2 * (s - 1) + layer) + k
                    act.wait_ge(ps_h, n + 1)
                    wait(act, lo_g, n - 1)
                    nc.scalar.activation(gf[:, k % 2, :], h_bank(s, layer, k)[:, :], ACT.Gelu, scale=hs[:, 2 + layer, k:k + 1]).then_inc(ev_h, 1)
                elif what == "wt_hi":
                    u = it[1]
                    act.wait_ge(ps_wt, u + 1)
                    nc.scalar.activation(wt_dst(u, 0), f_bank[u % 2][:, :], ACT.Copy).then_inc(hi_wt, 1)

        @block.vector
        def _(dve):
            def k_rows(j):
                rows = stack[1][:, GH * j:GH * (j + 1), :].rearrange("p h n -> p (h n)").bitcast(F32)
                nc.vector.memset(rows[32:64, :], 0.0).then_inc(ones, 1)
                nc.vector.memset(rows[64:P, :], TWO_ONES).then_inc(ones, 1)

            k_rows(0)
            k_rows(1)
            dve.wait_ge(ps_wq, 1)
            for i in range(3):
                nc.vector.tensor_copy(qkvT[:, i, :].rearrange("p (h d) -> p h d", d=HD),
                                      f_bank[0][:, 0:3 * D].rearrange("p (h k d) -> p k h d", k=3, d=HD)[:, i]).then_inc(ev_wq, 1)
            nc.vector.tensor_copy(fcT[:, :], f_bank[0][:, 3 * D:4 * D]).then_inc(ev_wq, 1)
            k_rows(2)
            k_rows(3)
            sums = t_bank[:, :].rearrange("p (a w) -> p a w", w=VW)

            def layernorm(k, count):
                b, second = count // 2, count % 2
                if k == 0 and not second:
                    dve.wait_ge(ps_fc, b + 1)
                    dve.wait_ge(resb, b + 1)
                    nc.vector.tensor_tensor(res[:, :, :].rearrange("p t c -> p (t c)"), f_bank[1][:, :],
                                            x_res[:, :, :].rearrange("p t c -> p (t c)"), ALU.add).then_inc(ln_step, 1)
                elif k == 0:
                    dve.wait_ge(ev_w3, b + 1)
                    nc.vector.tensor_tensor(res[:, :, :], res[:, :, :], x1[:, :, :], ALU.add).then_inc(ln_step, 1)
                elif k == 1:
                    dve.wait_ge(ln_step, 4 * count + 1)
                    for t in range(NT):
                        last = nc.vector.bn_stats(stats[:, t, :], res[:, t, :])
                    last.then_inc(ln_step, 1)
                elif k == 2:
                    dve.wait_ge(ln_step, 4 * count + 2)
                    for t in range(NT):
                        last = nc.vector.bn_aggr(mv[:, t, :], stats[:, t, :])
                    last.then_inc(ln_step, 1)
                elif k == 3:
                    dve.wait_ge(ln_step, 4 * count + 3)
                    nc.vector.tensor_scalar(rstd[:, 0, :], mv[:, :, 1], EPS, None, ALU.add).then_inc(ln_step, 1)
                else:
                    dve.wait_ge(rs_ok, count + 1)
                    if second:
                        wait(dve, st_out, 16 * b)
                    dst, done = ((x1, x1_ok), (y, y_ok))[second]
                    for t in range(NT):
                        last = nc.vector.tensor_scalar(dst[:, t, :], res[:, t, :], mv[:, t, 0:1], rstd[:, 1, t:t + 1],
                                                       ALU.subtract, ALU.mult)
                    last.then_inc(done, 1)

            def low_part(u):
                dve.wait_ge(ev_wt, u + 1)
                mx = nc.vector.tensor_reduce(wlow[:, u:u + 1], wt_dst(u, 1).bitcast(F32), AX.X, ALU.max,
                                             apply_absolute_value=True)
                if u == WT - 1:
                    mx.then_inc(lo_max, 1)

            for s, it in program(ALL):
                what = it[0]
                if what == "s":
                    mm = it[1]
                    m = BT * max(s, 0) + mm
                    c, qt = (m % GT) // NT, m % NT
                    g = m // GT
                    if m % GT == 0:
                        wait(dve, m_parts, g - 1)
                    dve.wait_ge(ps_s, m + 1)
                    nc.vector.tensor_reduce(negmax[:, g % 2, qt, c:c + 1], s_bank[m % 2][:, :], AX.X,
                                            ALU.max, negate=True).then_inc(ev_s, 1)
                elif what == "split":
                    b, k, i = s + 1, it[1], it[2]
                    n = 2 * b + i
                    pt = parts[i]
                    A, Bs, C = ((0, 1, 2), (3, 4), 5) if i == 0 else ((0, 3, 5), (1, 4), 2)
                    if k == 0:
                        dve.wait_ge(ev_qk, n + 1)
                        if b:
                            for h in range(H):
                                dve.wait_ge(rep[h], 16 * 2 * b)
                        nc.vector.tensor_copy(pt[:, A[0], :], qk_f[i][:, :]).then_inc(qk_step[i], 1)
                    elif k == 1:
                        dve.wait_ge(qk_step[i], 3 * b + 1)
                        nc.vector.tensor_tensor(qk_r[i][:, :], qk_f[i][:, :], pt[:, A[0], :], ALU.subtract).then_inc(qk_step[i], 1)
                        for a in A[1:]:
                            nc.vector.tensor_copy(pt[:, a, :], pt[:, A[0], :])
                    elif k == 2:
                        dve.wait_ge(qk_step[i], 3 * b + 2)
                        nc.vector.tensor_copy(pt[:, Bs[0], :], qk_r[i][:, :]).then_inc(qk_step[i], 1)
                    else:
                        dve.wait_ge(qk_step[i], 3 * b + 3)
                        nc.vector.tensor_copy(pt[:, Bs[1], :], pt[:, Bs[0], :])
                        nc.vector.tensor_tensor(pt[:, C, :], qk_r[i][:, :], pt[:, Bs[0], :], ALU.subtract).then_inc(qk_parts[i], 1)
                elif what == "v_in":
                    b = max(s, 0)
                    dve.wait_ge(ps_v, b + 1)
                    if b == 0:
                        dve.wait_ge(ld_vb, 16 * NT)
                        dve.wait_ge(vzero, 2)
                    wait(dve, ps_pv, NG * NT * b)
                    nc.vector.tensor_tensor(v_sb[:, :, :, 0:HD].rearrange("p t h d -> p (t h) d"),
                                            f_bank[0][:, :].rearrange("p (a d) -> p a d", d=HD),
                                            vb[:, :, :].rearrange("p t (h d) -> p (t h) d", d=HD), ALU.add).then_inc(ev_v, 1)
                elif what == "oT_rec":
                    g = NG * s + it[1]
                    dve.wait_ge(ps_oT, g + 1)
                    nc.vector.reciprocal(rden[:, :], sums[:, :, HD]).then_inc(rd_oT, 1)
                elif what == "oT_mul":
                    g = NG * s + it[1]
                    j = g % NG
                    dve.wait_ge(rd_oT, g + 1)
                    if j == 0:
                        wait(dve, ps_aT, g // NG)
                    for t in range(NT):
                        last = nc.vector.tensor_tensor(
                            attn[:, t, GH * HD * j:GH * HD * (j + 1)].rearrange("p (c d) -> p c d", d=HD),
                            sums[:, GH * t:GH * (t + 1), 0:HD],
                            rden[:, GH * t:GH * (t + 1)].unsqueeze(2).broadcast_to([P, GH, HD]), ALU.mult)
                    last.then_inc(ev_oT, 1)
                elif what == "ln":
                    layernorm(it[1], it[2])
                elif what == "x1T_hi":
                    dve.wait_ge(ps_x1T, s)
                    wait(dve, ps_w2, NK * (s - 1))
                    nc.vector.tensor_copy(x1T[0][:, :], t_bank[:, :]).then_inc(hi_x1T, 1)
                elif what == "x1T_lo":
                    dve.wait_ge(hi_x1T, s)
                    nc.vector.tensor_tensor(x1T[1][:, :], t_bank[:, :], x1T[0][:, :].bitcast(F32), ALU.subtract).then_inc(ev_x1T, 1)
                elif what == "w12":
                    k = it[1]
                    n = NK * (s - 1) + k
                    dve.wait_ge(ps_w2, n + 1)
                    dve.wait_ge(ev_w1, n + 1)
                    wait(dve, lo0, n - 1)
                    nc.vector.scalar_tensor_tensor(hf[:, k % 2, :], w2_bank(s, k)[:, :], hs[:, 1, k:k + 1], silu[:, k % 2, :],
                                                   ALU.mult, ALU.mult).then_inc(ev_w2, 1)
                elif what == "w12_lo":
                    k = it[1]
                    dve.wait_ge(hi0, NK * (s - 1) + k + 1)
                    nc.vector.tensor_tensor(act0[1][:, k, :], hf[:, k % 2, :], act0[0][:, k, :].bitcast(F32),
                                            ALU.subtract).then_inc(lo0, 1)
                elif what == "w12_hi":
                    k = it[1]
                    n = NK * (s - 1) + k
                    dve.wait_ge(ev_w2, n + 1)
                    if k == 0:
                        wait(dve, ps_w3, s - 1)
                    nc.vector.tensor_copy(act0[0][:, k, :], hf[:, k % 2, :]).then_inc(hi0, 1)
                elif what == "h":
                    layer, k = it[1], it[2]
                    n = NK * (2 * (s - 1) + layer) + k
                    dve.wait_ge(ev_h, n + 1)
                    if k == 0 and layer == 0:
                        wait(dve, ps_h, 2 * NK * (s - 1))
                    elif k == 0:
                        wait(dve, ps_h, NK * (2 * (s - 1) + 1))
                    a = (act1, act2)[layer]
                    nc.vector.tensor_copy(a[0][:, k, :], gf[:, k % 2, :]).then_inc(hi_g, 1)
                    if s == B:
                        dve.wait_ge(hi_g, n + 1)
                        nc.vector.tensor_tensor(a[1][:, k, :], gf[:, k % 2, :], a[0][:, k, :].bitcast(F32),
                                                ALU.subtract).then_inc(lo_g, 1)
                elif what == "w3_in":
                    dve.wait_ge(ps_w3, s)
                    if s < B:
                        nc.vector.tensor_tensor(res[:, :, :].rearrange("p t c -> p (t c)"), f_bank[0][:, :],
                                                s3[:, :, :].rearrange("p t c -> p (t c)"), ALU.mult).then_inc(ev_w3, 1)
                    else:
                        for t in range(NT):
                            last = nc.vector.tensor_tensor(res[:, t, :], last_banks[0][t][:, 0:P], s3[:, t, :], ALU.mult)
                        last.then_inc(ev_w3, 1)
                elif what == "wt_lo":
                    u = it[1]
                    dve.wait_ge(hi_wt, u + 1)
                    nc.vector.tensor_tensor(wt_dst(u, 1), f_bank[u % 2][:, :], wt_dst(u, 0).bitcast(F32), ALU.subtract).then_inc(ev_wt, 1)
                    if u:
                        low_part(u - 1)
                elif what == "w_low":
                    low_part(WT - 1)
                    dve.wait_ge(lo_max, 1)
                    nc.vector.tensor_reduce(wlow1[:, :], wlow[:, :], AX.X, ALU.max).then_inc(lo_max, 1)
                    dve.wait_ge(ps_low, 1)
                    nc.vector.tensor_reduce(wflag[:, :], f_bank[1][0:1, 0:P], AX.X, ALU.max).then_inc(low_ok, 1)

        @block.gpsimd
        def _(pool):
            nc.gpsimd.memset(ident[:, :], 0.0).then_inc(ids, 1)
            nc.gpsimd.memset(ident16[:, :], 0.0).then_inc(ids, 1)
            pool.wait_ge(ids, 2)
            for m in (ident, ident16):
                nc.gpsimd.affine_select(out=m[:, :], in_=m[:, :], compare_op=ALU.not_equal, fill=1.0, base=0,
                                        pattern=[[-1, P]], channel_multiplier=1).then_inc(ids, 1)
            pool.wait_ge(ids, 4)
            for j in range(NG):
                rows = stack[0][:, GH * j:GH * (j + 1), :].rearrange("p h n -> p (h n)").bitcast(F32)
                wait(pool, zeros, 2 * j)
                nc.gpsimd.memset(rows[32:64, :], 0.0).then_inc(zeros, 1)
                pool.wait_ge(zeros, 2 * j + 1)
                nc.gpsimd.memset(rows[64:P, :], 0.0).then_inc(zeros, 1)
            pool.wait_ge(zeros, 2 * NG)
            nc.gpsimd.memset(v_sb[:, :, :, :], 0.0).then_inc(vzero, 1)
            pool.wait_ge(vzero, 1)
            nc.gpsimd.memset(v_sb[:, :, :, HD:HD + 1], 1.0).then_inc(vzero, 1)

            nc.gpsimd.memset(mhalf[:, :], -0.5).then_inc(vzero, 1)

            def inv_sqrt(count):
                pool.wait_ge(ln_step, 4 * count + 4)
                if count == 0:
                    pool.wait_ge(vzero, 3)
                nc.gpsimd.tensor_tensor(rstd[:, 1, :], rstd[:, 0, :], mhalf[:, :], ALU.pow).then_inc(rs_ok, 1)

            for s, it in program(ALL):
                what = it[0]
                if what == "ln" and it[1] == 3:
                    inv_sqrt(it[2])
                elif what == "m_split":
                    g = NG * s + it[1] if s >= 0 else 0
                    pool.wait_ge(ev_s, GT * (g + 1))
                    wait(pool, ps_mT, g)
                    nm = negmax[:, g % 2]
                    nc.gpsimd.tensor_copy(mparts[:, :, 0, :], nm).then_inc(m_step, 1)
                    pool.wait_ge(m_step, 3 * g + 1)
                    nc.gpsimd.tensor_tensor(mres[:, :, :], nm, mparts[:, :, 0, :], ALU.subtract).then_inc(m_step, 1)
                    pool.wait_ge(m_step, 3 * g + 2)
                    nc.gpsimd.tensor_copy(mparts[:, :, 1, :], mres[:, :, :]).then_inc(m_step, 1)
                    pool.wait_ge(m_step, 3 * g + 3)
                    nc.gpsimd.tensor_tensor(mparts[:, :, 2, :], mres[:, :, :], mparts[:, :, 1, :],
                                            ALU.subtract).then_inc(m_parts, 1)
                elif what == "pv" and it[1] == 1 and it[2] == 0 and s < B:
                    if s == 0:
                        pool.wait_ge(ld_fcb, 16 * NT)
                    pool.wait_ge(ld_res, 16 * (s + 1))
                    nc.gpsimd.tensor_tensor(x_res[:, :, :], x_res[:, :, :], x_res[:, :, :], ALU.add).then_inc(res2, 1)
                    pool.wait_ge(res2, s + 1)
                    nc.gpsimd.tensor_tensor(x_res[:, :, :], x_res[:, :, :], fcb[:, :, :], ALU.add).then_inc(resb, 1)
                elif what == "w12_hi" and s < B:
                    k = it[1]
                    n = NK * (s - 1) + k
                    pool.wait_ge(hi0, n + 1)
                    nc.gpsimd.tensor_tensor(act0[1][:, k, :], hf[:, k % 2, :], act0[0][:, k, :].bitcast(F32),
                                            ALU.subtract).then_inc(lo0, 1)
                elif what == "h" and s < B:
                    layer, k = it[1], it[2]
                    n = NK * (2 * (s - 1) + layer) + k
                    pool.wait_ge(hi_g, n + 1)
                    a = (act1, act2)[layer]
                    nc.gpsimd.tensor_tensor(a[1][:, k, :], gf[:, k % 2, :], a[0][:, k, :].bitcast(F32),
                                            ALU.subtract).then_inc(lo_g, 1)


_INS = ['L0_attn_x', 'L0_attn_qkv_w', 'L0_attn_qkv_b', 'L0_attn_fc_w', 'L0_attn_fc_b', 'L0_ffn_w1_w', 'L0_ffn_w1_s',
        'L0_ffn_w2_w', 'L0_ffn_w2_s', 'L0_ffn_h1_w', 'L0_ffn_h1_s', 'L0_ffn_h2_w', 'L0_ffn_h2_s', 'L0_ffn_w3_w',
        'L0_ffn_w3_s']
_OUTS = [((4, 512, 128), 'float32')]


def kernel(**inputs):
    import numpy as _np
    import concourse.bacc as _bacc
    from concourse import mybir as _mybir
    from concourse.bass_utils import run_bass_kernel_spmd as _run

    nc = _bacc.Bacc("TRN2", target_bir_lowering=False, num_devices=1)
    arrays, args = {}, []
    for name in _INS:
        a = _np.ascontiguousarray(inputs[name])
        arrays[f"in_{name}_dram"] = a
        args.append(nc.dram_tensor(f"in_{name}_dram", a.shape, _mybir.dt.from_np(a.dtype), kind="ExternalInput").ap())
    for i, (shape, dtype) in enumerate(_OUTS):
        dt = _mybir.dt.from_np(_np.dtype(dtype))
        args.append(nc.dram_tensor(f"out_{i}_dram", shape, dt, kind="ExternalOutput").ap())
    post_ln_block_kernel(nc, *args)
    r = _run(nc, [arrays], core_ids=[0])
    got = tuple(r.results[0][f"out_{i}_dram"] for i in range(len(_OUTS)))
    return got[0]
```

```python
import numpy as np

import concourse.bass as bass
from concourse import mybir
from contextlib import ExitStack


def post_ln_block_kernel(
    nc: bass.Bass,
    x: bass.AP,
    qkv_w: bass.AP,
    qkv_b: bass.AP,
    fc_w: bass.AP,
    fc_b: bass.AP,
    w1_w: bass.AP,
    w1_s: bass.AP,
    w2_w: bass.AP,
    w2_s: bass.AP,
    h1_w: bass.AP,
    h1_s: bass.AP,
    h2_w: bass.AP,
    h2_s: bass.AP,
    w3_w: bass.AP,
    w3_s: bass.AP,
    out: bass.AP,
):
    F32, F32R, BF16 = mybir.dt.float32, mybir.dt.float32r, mybir.dt.bfloat16
    ALU = mybir.AluOpType
    ACT = mybir.ActivationFunctionType
    AX = mybir.AxisListType

    P = 128
    B, N, D = x.shape
    H = 16
    HD = D // H
    HID = w1_w.shape[0]
    SCALE = float(HD) ** -0.5
    EPS = 1e-5
    NT = N // P
    NK = HID // P
    GH = 4
    NG = H // GH
    GT = GH * NT
    BT = NG * GT
    NPART = 3
    SLOTS = 6
    SR = SLOTS * HD
    MROW = 96
    VW = 32
    LEAD = 28
    FIRST_LEAD, FIRST_MT = 28, 20
    TWO_ONES = float(np.array([0x3F803F80], np.uint32).view(np.float32)[0])
    WT = 3 + 2 * NK
    NS = 2
    NP = 8
    assert D == P and HID == 512 and N == 512 and H == 16

    with ExitStack() as ctx:
        def sb(name, shape, dt):
            return ctx.enter_context(nc.sbuf_tensor(name, shape, dt))

        def sem(name):
            return ctx.enter_context(nc.semaphore(name))

        def bank(name):
            return ctx.enter_context(nc.psum_tensor(name, [P, 512], F32))

        s_bank = [bank(f"s_bank{i}") for i in range(NS)]
        st_bank = [bank(f"st_bank{i}") for i in range(3)]
        pv_bank = bank("pv_bank")
        f_bank = [bank(f"f_bank{i}") for i in range(2)]
        t_bank = f_bank[1]
        t_bank16 = t_bank[:, :].bitcast(BF16)

        ident = sb("ident", [P, P], F32)
        ident16 = sb("ident16", [P, P], BF16)
        h1_nat = sb("h1_nat", [P, NK, HID], F32)
        work = sb("work", [P, 6, N], F32)
        y = sb("y", [P, NT, D], F32)
        res = sb("res", [P, NT, D], F32)
        qkv_nat, fc_nat = res[:, 0:3, :], res[:, 3, :]
        h_nat = [h1_nat[:, :, :], work[:, 0:4, :]]
        w_nat = work[:, 4:6, :].rearrange("p w (t c) -> p w t c", t=NK)
        w3_nat = y[:, :, :].rearrange("p t c -> p (t c)")
        qkvT = sb("qkvT", [P, 3, D], F32)
        fcT = sb("fcT", [P, D], F32)
        w12T = [sb(f"w12T{i}", [P, 2, HID], F32R) for i in range(2)]
        hT = [sb(f"hT{i}", [P, 2 * NK, HID], F32R) for i in range(2)]
        w3T = [sb(f"w3T{i}", [P, NK, D], F32R) for i in range(2)]
        qkb = sb("qkb", [P, 2], F32)
        vb = sb("vb", [P, NT, D], F32)
        fcb = sb("fcb", [P, NT, D], F32)
        s3 = sb("s3", [P, 1], F32)
        mlpT = sb("mlpT", [P, N], F32)
        hs = sb("hs", [P, 4, NK], F32)

        x_in = sb("x_in", [P, NT, D], F32)
        x_res = sb("x_res", [P, NT, D], F32)
        xT = sb("xT", [P, N], F32)
        qk_f = [sb(f"qk_f{i}", [P, N], F32) for i in range(2)]
        qk_r = [sb(f"qk_r{i}", [P, N], F32) for i in range(2)]
        parts = [sb(f"parts{i}", [P, SLOTS, N], BF16) for i in range(2)]
        stack = [sb(f"stack{i}", [P, H, N], BF16) for i in range(2)]
        v_sb = sb("v_sb", [P, NT, H, VW], F32)
        negmax = sb("negmax", [P, 2, GH, NT], F32)
        mres = sb("mres", [P, GH, NT], F32)
        mparts = sb("mparts", [P, NPART, GH, NT], BF16)
        mT = sb("mT", [NPART * GH * NT, P], BF16)
        prob = sb("prob", [P, NP, N], F32)
        oT = sb("oT", [P, N], F32)
        rden = sb("rden", [P, NT * GH], F32)
        attn = sb("attn", [P, NT, D], F32)
        aT = sb("aT", [P, N], F32)
        warm = sb("warm", [P, 1], F32)
        stats = sb("stats", [P, NT, 6], F32)
        mv = sb("mv", [P, NT, 2], F32)
        rstd = sb("rstd", [P, 2, NT], F32)
        mhalf = sb("mhalf", [P, NT], F32)
        wlow = sb("wlow", [P, WT], F32)
        wlow1 = sb("wlow1", [P, 1], F32)
        wflag = sb("wflag", [1, 1], F32)
        x1 = sb("x1", [P, NT, D], F32)
        x1T = [sb(f"x1T{i}", [P, N], F32R) for i in range(2)]
        silu, hf, gf = work[:, 0:2, :], work[:, 2:4, :], work[:, 4:6, :]
        act0 = [sb(f"act0_{i}", [P, NK, N], F32R) for i in range(2)]
        act1 = [sb(f"act1_{i}", [P, NK, N], F32R) for i in range(2)]
        act2 = act0

        ld_qkv, ld_qkb, ld_vb, ld_fcb, ld_x, ld_res, ld_w, ld_h, ld_w3, ld_s = (
            sem(n) for n in ("ld_qkv", "ld_qkb", "ld_vb", "ld_fcb", "ld_x", "ld_res", "ld_w", "ld_h", "ld_w3", "ld_s"))
        st_out = sem("st_out")
        ids, ones, zeros, vzero = sem("ids"), sem("ones"), sem("zeros"), sem("vzero")
        ps_wq, ev_wq = sem("ps_wq"), sem("ev_wq")
        ps_wt, hi_wt, ev_wt = sem("ps_wt"), sem("hi_wt"), sem("ev_wt")
        ps_xT, ev_xT = sem("ps_xT"), sem("ev_xT")
        ps_qk, ev_qk = sem("ps_qk"), sem("ev_qk")
        qk_step, qk_parts = ([sem(f"{n}{i}") for i in range(2)] for n in ("qk_step", "qk_parts"))
        ps_v, ev_v = sem("ps_v"), sem("ev_v")
        rep = [sem(f"rep{h}") for h in range(H)]
        ps_s, ev_s = sem("ps_s"), sem("ev_s")
        m_step, m_parts, ps_mT, ev_mT = (sem(n) for n in ("m_step", "m_parts", "ps_mT", "ev_mT"))
        mrow = [sem(f"mrow{j}") for j in range(NG)]
        ps_st, ev_st, ps_pv = sem("ps_st"), sem("ev_st"), sem("ps_pv")
        ev_pv, ps_oT, rd_oT, ev_oT = (sem(n) for n in ("ev_pv", "ps_oT", "rd_oT", "ev_oT"))
        ps_aT, ev_aT, ps_fc = (sem(n) for n in ("ps_aT", "ev_aT", "ps_fc"))
        lo_max, ps_low, low_ok = sem("lo_max"), sem("ps_low"), sem("low_ok")
        res2, resb = sem("res2"), sem("resb")
        rs_ok = sem("rs_ok")
        ln_step, x1_ok, y_ok = sem("ln_step"), sem("x1_ok"), sem("y_ok")
        ps_x1T, hi_x1T, ev_x1T = sem("ps_x1T"), sem("hi_x1T"), sem("ev_x1T")
        ps_w1, ps_w2, ev_w1, ev_w2 = (sem(n) for n in ("ps_w1", "ps_w2", "ev_w1", "ev_w2"))
        hi0, lo0 = sem("hi0"), sem("lo0")
        ps_h, ev_h, hi_g, lo_g = (sem(n) for n in ("ps_h", "ev_h", "hi_g", "lo_g"))
        ps_w3, ev_w3, ps_w3T = sem("ps_w3"), sem("ev_w3"), sem("ps_w3T")

        def wait(eng, s, value):
            if not isinstance(value, int) or value > 0:
                eng.wait_ge(s, value)

        PLACE = {
            "pv3": [3, 17, 33, 50],
            "oT_in": [4, 21, 38, 51],
            "oT": [10, 23, 39, 54],
            "oT_rec": [11, 24, 40, 56],
            "oT_mul": [12, 25, 42, 57],
            "pv0": [7, 23, 39, 55],
            "pv1": [9, 27, 41, 55],
            "pv2": [15, 30, 47, 61],
            "m_split": [9, 24, 40, 57],
            "mT": [13, 27, 44, 58],
            "mT_in": [14, 28, 45, 60],
            "v": [0],
            "v_in": [4],
            "aT": [15],
            "aT_in": [16],
            "fc": [17],
            "ln1": [18, 19, 21, 22, 24],
            "x1T": [30],
            "x1T_hi": [31],
            "x1T_lo": [32],
            "w12": [33, 33, 33, 33],
            "h": [43, 43, 43, 43, 49, 49, 49, 49],
            "w3": [57],
            "w3_in": [60],
            "w3T": [62],
            "ln2": [63, 63, 2, 4, 6],
            "xT": [3],
            "xT_in": [5],
            "qk": [6, 8],
            "qk_in": [8, 9],
            "split": [10, 12, 11, 12, 13, 14, 14, 15],
            "spread": [16, 32, 48, 3],
            "wt": [17, 21, 25, 29, 33, 37, 41, 46, 49, 52, 57],
            "wt_hi": [18, 22, 26, 30, 34, 38, 43, 47, 50, 55, 58],
            "wt_lo": [19, 23, 28, 31, 35, 39, 44, 48, 51, 56, 59],
            "w_low": [62],
        }
        W12_US, H_US = 0.86, 1.24
        LN_STEPS = 5

        def order(s):
            now, nxt, prev = s < B, s + 1 < B, s >= 1
            at = {}

            def put(name, n, cost, *item):
                at.setdefault(PLACE[name][n], []).append((cost, item))

            for j in range(NG if now else 1):
                if j or prev:
                    put("pv3", j, 0.9, "pv", j - 1, 3)
                    put("oT_in", j, 0, "oT_in", j - 1)
                    put("oT", j, 0.44, "oT", j - 1)
                    put("oT_rec", j, 0, "oT_rec", j - 1)
                    put("oT_mul", j, 0, "oT_mul", j - 1)
                if now:
                    for k in range(NT - 1):
                        put(f"pv{k}", j, 0.9, "pv", j, k)
                    if j < NG - 1 or nxt:
                        put("m_split", j, 0, "m_split", j + 1)
                        put("mT", j, 0.22, "mT", j + 1)
                        put("mT_in", j, 0, "mT_in", j + 1)
            if prev:
                if now:
                    put("v", 0, 0.9, "v")
                    put("v_in", 0, 0, "v_in")
                put("aT", 0, 0.44, "aT")
                put("aT_in", 0, 0, "aT_in")
                put("fc", 0, 0.9, "fc")
                for k in range(LN_STEPS):
                    put("ln1", k, 0, "ln", k, 2 * (s - 1))
                put("x1T", 0, 0.44, "x1T")
                put("x1T_hi", 0, 0, "x1T_hi")
                put("x1T_lo", 0, 0, "x1T_lo")
                for k in range(NK):
                    put("w12", k, W12_US, "w12", k)
                    if now and k:
                        put("w12", k, 0, "w12_hi", k - 1)
                    elif not now:
                        if k:
                            put("w12", k, 0, "w12_lo", k - 1)
                        put("w12", k, 0, "w12_hi", k)
                put("w12", NK - 1, 0, *(("w12_hi" if now else "w12_lo"), NK - 1))
                for layer in range(2):
                    if not now:
                        put("h", 4 * layer, 0, "layer", layer)
                    for k in range(NK):
                        put("h", 4 * layer + k, H_US, "h", layer, k)
                put("w3", 0, 1.73, "w3")
                put("w3_in", 0, 0, "w3_in")
                put("w3T", 0, 0.44, "w3T")
                for k in range(LN_STEPS if not now else 2):
                    put("ln2", min(k, 1), 0, "ln", k, 2 * (s - 1) + 1)
            if s >= 2:
                for k in range(2, LN_STEPS):
                    put("ln2", k, 0, "ln", k, 2 * (s - 2) + 1)
            if nxt:
                put("xT", 0, 0.44, "xT")
                put("xT_in", 0, 0, "xT_in")
                for i in range(2):
                    put("qk", i, 0.9, "qk", i)
                for i in range(2):
                    put("qk_in", i, 0, "qk_in", i)
                for k in range(4):
                    for i in range(2):
                        put("split", 2 * k + i, 0, "split", k, i)
                for j in range(NG - 1):
                    put("spread", j, 0, "spread", j)
            if s == 0:
                for u in range(WT):
                    put("wt", u, 0.44, "wt", u)
                    put("wt_hi", u, 0, "wt_hi", u)
                    put("wt_lo", u, 0, "wt_lo", u)
                put("w_low", 0, 0.1, "w_low")
            if prev and now:
                put("spread", NG - 1, 0, "spread", NG - 1)

            items = []
            for j in range(NG):
                for i in range(GT):
                    if now:
                        items.append((0.22, ("st", j, i)))
                    items += at.get(GT * j + i, [])
            if not now:
                return [it for _, it in items]
            first = LEAD if s else FIRST_LEAD
            tiles = BT + LEAD - first
            total = sum(c for c, _ in items)
            placed, t, r = [], 0.0, 0
            for c, it in items:
                while r < tiles and t >= total * r / tiles:
                    if s * BT + first + r < B * BT:
                        placed.append(("s", first + r))
                    r += 1
                if it[0] == "m_split":
                    while first + r < (it[1] + 1) * GT and r < tiles:
                        placed.append(("s", first + r))
                        r += 1
                placed.append(it)
                t += c
            while r < tiles and s * BT + first + r < B * BT:
                placed.append(("s", first + r))
                r += 1
            return placed

        def prologue():
            return ([("xT",), ("xT_in",), ("qk", 0), ("qk", 1), ("qk_in", 0), ("qk_in", 1)]
                    + [("split", k, i) for i in range(2) for k in range(4)] + [("spread", j) for j in range(2)]
                    + [("v",)] + [("s", m) for m in range(GT)] + [("m_split", 0)] + [("s", m) for m in range(GT, FIRST_MT)]
                    + [("mT", 0), ("mT_in", 0)] + [("s", m) for m in range(FIRST_MT, FIRST_LEAD)] + [("v_in",)]
                    + [("spread", j) for j in range(2, NG)])

        def program(slots):
            for s in slots:
                for it in (order(s) if s >= 0 else prologue()):
                    yield s, it

        ALL = range(-1, B + 1)

        last_banks = [s_bank[0:2] + st_bank[:2], f_bank + [pv_bank, st_bank[2]]]

        def w1_bank(s, k):
            return last_banks[0][k] if s == B else f_bank[0]

        def w2_bank(s, k):
            return last_banks[1][k] if s == B else f_bank[1]

        def h_bank(s, layer, k):
            return last_banks[layer][k] if s == B else f_bank[k % 2]

        block = ctx.enter_context(nc.Block())

        @block.sync
        def _(sp):
            sp.dma_start(x_in[:, :, :], x[0].rearrange("(t p) c -> p t c", p=P)).then_inc(ld_x, 16)
            sp.dma_start(qkv_nat, qkv_w.rearrange("(t p) c -> p t c", p=P)).then_inc(ld_qkv, 16)
            sp.dma_start(fc_nat, fc_w).then_inc(ld_qkv, 16)
            qkv_bh = qkv_b.rearrange("(h k d) -> k h d", k=3, d=HD)
            for i in range(2):
                sp.dma_start(qkb[:, i:i + 1], qkv_bh[i]).then_inc(ld_qkb, 16)

            def more_loads():
                for i, w in enumerate((w1_w, w2_w)):
                    sp.dma_start(w_nat[:, i, :, :], w.rearrange("(t p) c -> p t c", p=P)).then_inc(ld_w, 16)
                for i, w in enumerate((h1_w, h2_w)):
                    sp.dma_start(h_nat[i], w.rearrange("(t p) c -> p t c", p=P)).then_inc(ld_h, 16)
                sp.dma_start(w3_nat, w3_w).then_inc(ld_w3, 16)
                sp.dma_start(x_res[:, :, :], x[0].rearrange("(t p) c -> p t c", p=P)).then_inc(ld_res, 16)
                for t in range(NT):
                    sp.dma_start(fcb[:, t, :], fc_b.partition_broadcast(P)).then_inc(ld_fcb, 16)
                sp.dma_start(s3[:, :], w3_s.unsqueeze(1)).then_inc(ld_s, 16)
                for i, w in enumerate((w1_s, w2_s, h1_s, h2_s)):
                    sp.dma_start(hs[:, i, :], w.rearrange("(k p) -> p k", p=P),
                                 allow_slow_non_contiguous=True).then_inc(ld_s, 16)

            for t in range(NT):
                sp.dma_start(vb[:, t, :].rearrange("p (h d) -> p h d", d=HD),
                             qkv_bh[2].partition_broadcast(P)).then_inc(ld_vb, 16)

            def spread(b, j):
                if b == 0:
                    wait(sp, ones, 2 * (j + 1))
                    wait(sp, zeros, 2 * (j + 1))
                wait(sp, ps_st, BT * (b - 1) + GT * (j + 1))
                for i in range(2):
                    wait(sp, qk_parts[i], b + 1)
                    for h in range(GH * j, GH * (j + 1)):
                        sp.dma_start(stack[i][0:SR, h, :],
                                     parts[i][HD * h:HD * h + HD, :, :]).then_inc(rep[h], 16)

            for s, it in program(ALL):
                if it[0] == "xT_in" and s + 2 < B:
                    wait(sp, ps_xT, s + 2)
                    sp.dma_start(x_in[:, :, :], x[s + 2].rearrange("(t p) c -> p t c", p=P)).then_inc(ld_x, 16)
                elif it[0] == "spread":
                    j = it[1]
                    spread(s if s >= 0 and j == NG - 1 else s + 1, j)
                elif it[0] == "mT_in":
                    g = NG * s + it[1] if s >= 0 else 0
                    wait(sp, ev_mT, g + 1)
                    j = it[1] % NG
                    sp.dma_start(stack[0][MROW:MROW + NPART, GH * j:GH * (j + 1), :], mT[:, :]).then_inc(mrow[j], 16)
                    if s == -1:
                        more_loads()
                elif it[0] == "ln" and it[1] == 2 and it[2] % 2 == 0 and s < B:
                    wait(sp, ln_step, 8 * (s - 1) + 1)
                    sp.dma_start(x_res[:, :, :], x[s].rearrange("(t p) c -> p t c", p=P)).then_inc(ld_res, 16)
                elif it[0] == "ln" and it[1] == 4 and it[2] % 2 == 1:
                    b = it[2] // 2
                    wait(sp, y_ok, b + 1)
                    sp.dma_start(out[b].rearrange("(t p) c -> p t c", p=P), y[:, :, :]).then_inc(st_out, 16)
            sp.wait_ge(st_out, 16 * B)

        @block.tensor
        def _(pe):
            def transpose4(dst, src):
                for t in range(4):
                    last = nc.tensor.transpose(dst[:, t * P:(t + 1) * P], src(t), ident[:, :])
                return last

            pe.wait_ge(ids, 4)
            pe.wait_ge(ld_qkv, 32)
            for t in range(3):
                nc.tensor.transpose(f_bank[0][:, t * P:(t + 1) * P], qkv_nat[:, t, :], ident[:, :])
            nc.tensor.transpose(f_bank[0][:, 3 * P:4 * P], fc_nat, ident[:, :]).then_inc(ps_wq, 1)

            def scores_q(m, b):
                j, c, qt = m // GT, (m % GT) // NT, m % NT
                h = GH * j + c
                if qt == 0:
                    wait(pe, rep[h], 16 * 2 * (b + 1))
                wait(pe, ev_s, b * BT + m + 1 - NS)
                nc.tensor.matmul(s_bank[(b * BT + m) % NS][:, :], stack[0][0:MROW, h, qt * P:(qt + 1) * P],
                                 stack[1][0:MROW, h, :], start=True, stop=True).then_inc(ps_s, 1)

            def scores_k(n, b):
                j, kt, c = n // GT, (n % GT) // GH, n % GH
                h = GH * j + c
                if n % GT == 0:
                    wait(pe, mrow[j], 16 * (b + 1))
                wait(pe, ev_st, b * BT + n - 2)
                nc.tensor.matmul(st_bank[(b * BT + n) % 3][:, :], stack[1][:, h, kt * P:(kt + 1) * P], stack[0][:, h, :], start=True, stop=True).then_inc(ps_st, 1)

            def pv(g, kt):
                wait(pe, ev_st, (NT * g + kt + 1) * GH)
                if kt == 0:
                    wait(pe, ev_pv, g)
                    wait(pe, ev_v, g // NG + 1)
                j = g % NG
                for c in range(GH):
                    last = nc.tensor.matmul(pv_bank[VW * c:VW * c + VW, :], v_sb[:, kt, GH * j + c, :],
                                            prob[:, (GH * kt + c) % NP, :], start=kt == 0, stop=kt == NT - 1)
                last.then_inc(ps_pv, 1)

            def split_mm(dst, lefts, rights, first, last):
                pairs = [(w, v) for w in lefts for v in rights]
                for n, (w, v) in enumerate(pairs):
                    mm = nc.tensor.matmul(dst, w, v, start=first and n == 0, stop=last and n == len(pairs) - 1)
                return mm

            def step(s, it, wparts):
                what = it[0]
                if what == "s":
                    m = it[1]
                    scores_q(m % BT, max(s, 0) + m // BT)
                elif what == "st":
                    scores_k(GT * it[1] + it[2], s)
                elif what == "pv":
                    pv(NG * s + it[1], it[2])
                elif what == "xT":
                    b = s + 1
                    wait(pe, ld_x, 16 * (b + 1))
                    if s >= 2:
                        wait(pe, ln_step, 8 * (s - 2) + 5)
                    elif s >= 0:
                        wait(pe, ev_mT, NG * s + 1)
                    transpose4(t_bank, lambda t: x_in[:, t, :]).then_inc(ps_xT, 1)
                elif what == "qk":
                    b, i = s + 1, it[1]
                    wait(pe, ev_xT, b + 1)
                    if s == -1:
                        wait(pe, ev_wq, 4)
                    elif i == 0:
                        wait(pe, ev_v, s + 1)
                    nc.tensor.matmul(f_bank[i][:, :], qkvT[:, i, :], xT[:, :], start=True, stop=True).then_inc(ps_qk, 1)
                elif what == "v":
                    b = max(s, 0)
                    wait(pe, ev_xT, b + 1)
                    if s >= 2:
                        wait(pe, ev_w3, s - 1)
                    elif s == 1:
                        wait(pe, ev_wt, WT)
                    else:
                        wait(pe, ev_qk, 1)
                    for t in range(NT):
                        last = nc.tensor.matmul(f_bank[0][:, t * P:(t + 1) * P], xT[:, t * P:(t + 1) * P],
                                                qkvT[:, 2, :], start=True, stop=True)
                    last.then_inc(ps_v, 1)
                elif what == "mT":
                    g = NG * s + it[1] if s >= 0 else 0
                    wait(pe, m_parts, g + 1)
                    if g < 2:
                        wait(pe, ev_qk, 2 * (g + 1))
                    elif s >= 1 and it[1] == 3:
                        wait(pe, ev_h, NK * (2 * s - 1))
                    else:
                        wait(pe, ev_oT, g - 1)
                    nc.tensor.transpose(t_bank16[0:NPART * GT, 0:P],
                                        mparts[:, :, :, :].rearrange("p m c t -> p (m c t)"), ident16[:, :]).then_inc(ps_mT, 1)
                elif what == "oT":
                    g = NG * s + it[1]
                    wait(pe, ev_pv, g + 1)
                    j = it[1]
                    if j == -1 and s + 1 < B:
                        wait(pe, ev_qk, 2 * (s + 2))
                    elif j == -1:
                        wait(pe, ln_step, 8 * (s - 2) + 5)
                    elif j == 0 and s >= 1:
                        wait(pe, ev_aT, s)
                    elif j == 1 and s >= 1:
                        wait(pe, ev_w2, NK * s)
                    elif j == 2 and s >= 1:
                        wait(pe, ev_h, 2 * NK * s)
                    else:
                        wait(pe, ev_mT, g + 2)
                    transpose4(t_bank, lambda t: oT[:, t * P:(t + 1) * P]).then_inc(ps_oT, 1)
                elif what == "aT":
                    wait(pe, ev_oT, NG * s)
                    if s < B:
                        wait(pe, ev_mT, NG * s + 2)
                    transpose4(t_bank, lambda t: attn[:, t, :]).then_inc(ps_aT, 1)
                elif what == "fc":
                    wait(pe, ev_aT, s)
                    if s + 1 < B:
                        wait(pe, ev_qk, 2 * (s + 1) + 1)
                    elif s < B:
                        wait(pe, ev_v, s + 1)
                    else:
                        wait(pe, ev_w3, s - 1)
                    for t in range(NT):
                        last = nc.tensor.matmul(f_bank[0][:, t * P:(t + 1) * P], aT[:, t * P:(t + 1) * P],
                                                fcT[:, :], start=True, stop=True)
                    last.then_inc(ps_fc, 1)
                elif what == "x1T":
                    wait(pe, x1_ok, s)
                    if s < B:
                        wait(pe, ev_mT, NG * s + 3)
                    else:
                        wait(pe, ev_aT, s)
                    transpose4(t_bank, lambda t: x1[:, t, :]).then_inc(ps_x1T, 1)
                elif what == "w12":
                    k = it[1]
                    cols = slice(k * P, (k + 1) * P)
                    if k == 0:
                        wait(pe, ev_x1T, s)
                        wait(pe, ev_wt, WT)
                        wait(pe, ln_step, 8 * (s - 1) + 1)
                    elif s < B:
                        wait(pe, ev_w1, NK * (s - 1) + k)
                    if s == B and k == 0:
                        wait(pe, ev_s, B * BT)
                        wait(pe, ev_st, B * BT)
                        wait(pe, ev_pv, B * NG)
                    xs = [x1T[0][:, :], x1T[1][:, :]]
                    split_mm(w1_bank(s, k)[:, :], [w[:, 0, cols] for w in w12T[:wparts]], xs, True, True).then_inc(ps_w1, 1)
                    if k and s < B:
                        wait(pe, ev_w2, NK * (s - 1) + k)
                    split_mm(w2_bank(s, k)[:, :], [w[:, 1, cols] for w in w12T[:wparts]], xs, True, True).then_inc(ps_w2, 1)
                elif what == "layer":
                    layer = it[1]
                    src = (act0, act1)[layer]
                    hi, lo = ((hi0, lo0), (hi_g, lo_g))[layer]
                    before = NK * (B - 1) if layer == 0 else NK * 2 * (B - 1)
                    wait(pe, (ev_w1, ev_w2)[layer], NK * B)
                    for kk in range(NK):
                        halves = [[0], [1]] if kk < NK - 1 else [[0, 1]]
                        for half in halves:
                            if 0 in half:
                                wait(pe, hi, before + kk + 1)
                            if 1 in half:
                                wait(pe, lo, before + kk + 1)
                            for k in range(NK):
                                last = split_mm(last_banks[layer][k][:, :],
                                                [w[:, NK * layer + kk, k * P:(k + 1) * P] for w in hT[:wparts]],
                                                [src[i][:, kk, :] for i in half],
                                                kk == 0 and 0 in half, kk == NK - 1)
                                if kk == NK - 1:
                                    last.then_inc(ps_h, 1)
                elif what == "h" and s < B:
                    layer, k = it[1], it[2]
                    cols = slice(k * P, (k + 1) * P)
                    done = NK * (2 * (s - 1) + layer)
                    src = (act0, act1)[layer]
                    if k == 0:
                        wait(pe, hi0 if layer == 0 else hi_g, (NK * s) if layer == 0 else done)
                        wait(pe, lo0 if layer == 0 else lo_g, (NK * s) if layer == 0 else done)
                    if layer == 0 and k < 2:
                        wait(pe, (ev_w1, ev_oT)[k], NK * s if k == 0 else NG * s + 2)
                    elif k == 1:
                        wait(pe, ev_mT, NG * s + 4)
                    else:
                        wait(pe, ev_h, done + k - 1)
                    for kk in range(NK):
                        last = split_mm(f_bank[k % 2][:, :], [w[:, NK * layer + kk, cols] for w in hT[:wparts]],
                                        [a[:, kk, :] for a in src], kk == 0, kk == NK - 1)
                    last.then_inc(ps_h, 1)
                elif what == "w3" and s == B:
                    wait(pe, ev_h, NK * (2 * B - 1))
                    for kk in range(NK):
                        for i, part in enumerate((hi_g, lo_g)):
                            wait(pe, part, NK * (2 * B - 1) + kk + 1)
                            last = split_mm(last_banks[0][0][:, :], [w[:, kk, :] for w in w3T[:wparts]],
                                            [act2[i][:, kk, :]], kk == 0 and i == 0, kk == NK - 1 and i == 1)
                    last.then_inc(ps_w3, 1)
                elif what == "w3":
                    wait(pe, hi_g, 2 * NK * s)
                    wait(pe, lo_g, 2 * NK * s)
                    wait(pe, ev_h, 2 * NK * s - 1)
                    for kk in range(NK):
                        last = split_mm(f_bank[0][:, :], [w[:, kk, :] for w in w3T[:wparts]],
                                        [a[:, kk, :] for a in act2], kk == 0, kk == NK - 1)
                    last.then_inc(ps_w3, 1)
                elif what == "w3T":
                    wait(pe, ev_w3, s)
                    if s + 1 < B:
                        wait(pe, ev_mT, NG * s + 5)
                    elif s < B:
                        wait(pe, ev_oT, NG * s + 3)
                    else:
                        wait(pe, ev_h, 2 * NK * B)
                    transpose4(t_bank, lambda t: mlpT[:, t * P:(t + 1) * P]).then_inc(ps_w3T, 1)
                elif what == "wt":
                    u = it[1]
                    if u == 0:
                        wait(pe, ev_qk, 3)
                    wait(pe, ev_wt, u)
                    bank_ = f_bank[0]
                    if u < 2:
                        wait(pe, ld_w, 32)
                        last = transpose4(bank_, lambda t: w_nat[:, u, t, :])
                    elif u < 2 + 2 * NK:
                        wait(pe, ld_h, 32)
                        layer, kk = (u - 2) // NK, (u - 2) % NK
                        last = transpose4(bank_, lambda t: h_nat[layer][:, t, kk * P:(kk + 1) * P])
                    else:
                        wait(pe, ld_w3, 16)
                        last = transpose4(bank_, lambda t: w3_nat[:, t * P:(t + 1) * P])
                    last.then_inc(ps_wt, 1)
                elif what == "w_low":
                    wait(pe, lo_max, 2)
                    nc.tensor.transpose(f_bank[0][0:1, 0:P], wlow1[:, :], ident[:, :]).then_inc(ps_low, 1)

            for s, it in program(range(-1, 1)):
                step(s, it, 2)
            pe.wait_ge(low_ok, 1)
            low = pe.value_load(wflag[:, :].bitcast(mybir.dt.int32))
            with pe.If(low == 0):
                for s, it in program(range(1, B + 1)):
                    step(s, it, 1)
            with pe.Else():
                for s, it in program(range(1, B + 1)):
                    step(s, it, 2)

        def wt_dst(u, part):
            if u < 2:
                return w12T[part][:, u, :]
            if u < 2 + 2 * NK:
                return hT[part][:, u - 2, :]
            return w3T[part][:, :, :].rearrange("p k c -> p (k c)")

        @block.scalar
        def _(act):
            act.wait_ge(ids, 4)
            nc.scalar.activation(warm[:, :], ident[:, 0:1], ACT.Exp)
            act.wait_ge(ld_qkb, 32)
            for s, it in program(ALL):
                what = it[0]
                if what == "st":
                    r = GT * it[1] + it[2]
                    n = BT * s + r
                    if n % GH == 0:
                        wait(act, ps_pv, n // GH - 1)
                    act.wait_ge(ps_st, n + 1)
                    nc.scalar.activation(prob[:, r % NP, :], st_bank[n % 3][:, :], ACT.Exp, scale=SCALE).then_inc(ev_st, 1)
                elif what == "xT_in":
                    act.wait_ge(ps_xT, s + 2)
                    if s >= 0:
                        act.wait_ge(ps_v, s + 1)
                    nc.scalar.activation(xT[:, :], t_bank[:, :], ACT.Copy).then_inc(ev_xT, 1)
                elif what == "qk_in":
                    b, i = s + 1, it[1]
                    act.wait_ge(ps_qk, 2 * b + i + 1)
                    wait(act, qk_parts[i], b)
                    nc.scalar.activation(qk_f[i][:, :], f_bank[i][:, :], ACT.Identity, bias=qkb[:, i:i + 1]).then_inc(ev_qk, 1)
                elif what == "mT_in":
                    g = NG * s + it[1] if s >= 0 else 0
                    act.wait_ge(ps_mT, g + 1)
                    if g:
                        act.wait_ge(mrow[(g - 1) % NG], 16 * ((g - 1) // NG + 1))
                    nc.scalar.activation(mT[:, :], t_bank16[0:NPART * GT, 0:P], ACT.Copy).then_inc(ev_mT, 1)
                elif what == "oT_in":
                    g = NG * s + it[1]
                    act.wait_ge(ps_pv, NT * (g + 1))
                    wait(act, ps_oT, g)
                    nc.scalar.activation(oT[:, :], pv_bank[:, :], ACT.Copy).then_inc(ev_pv, 1)
                elif what == "aT_in":
                    act.wait_ge(ps_aT, s)
                    wait(act, ps_fc, s - 1)
                    nc.scalar.activation(aT[:, :], t_bank[:, :], ACT.Copy).then_inc(ev_aT, 1)
                elif what == "w12":
                    k = it[1]
                    n = NK * (s - 1) + k
                    if n == 0:
                        act.wait_ge(ld_s, 16 * 5)
                    act.wait_ge(ps_w1, n + 1)
                    wait(act, ev_w2, n - 1)
                    nc.scalar.activation(silu[:, k % 2, :], w1_bank(s, k)[:, :], ACT.Silu, scale=hs[:, 0, k:k + 1]).then_inc(ev_w1, 1)
                elif what == "h":
                    layer, k = it[1], it[2]
                    n = NK * (2 * (s - 1) + layer) + k
                    act.wait_ge(ps_h, n + 1)
                    wait(act, lo_g, n - 1)
                    nc.scalar.activation(gf[:, k % 2, :], h_bank(s, layer, k)[:, :], ACT.Gelu, scale=hs[:, 2 + layer, k:k + 1]).then_inc(ev_h, 1)
                elif what == "w3_in":
                    act.wait_ge(ps_w3, s)
                    wait(act, ps_w3T, s - 1)
                    src = last_banks[0][0] if s == B else f_bank[0]
                    nc.scalar.activation(mlpT[:, :], src[:, :], ACT.Copy, scale=s3[:, :]).then_inc(ev_w3, 1)
                elif what == "wt_hi":
                    u = it[1]
                    act.wait_ge(ps_wt, u + 1)
                    nc.scalar.activation(wt_dst(u, 0), f_bank[0][:, :], ACT.Copy).then_inc(hi_wt, 1)

        @block.vector
        def _(dve):
            def k_rows(j):
                rows = stack[1][:, GH * j:GH * (j + 1), :].rearrange("p h n -> p (h n)").bitcast(F32)
                nc.vector.memset(rows[32:64, :], 0.0).then_inc(ones, 1)
                nc.vector.memset(rows[64:P, :], TWO_ONES).then_inc(ones, 1)

            k_rows(0)
            k_rows(1)
            dve.wait_ge(ps_wq, 1)
            for i in range(3):
                nc.vector.tensor_copy(qkvT[:, i, :].rearrange("p (h d) -> p h d", d=HD),
                                      f_bank[0][:, 0:3 * D].rearrange("p (h k d) -> p k h d", k=3, d=HD)[:, i]).then_inc(ev_wq, 1)
            nc.vector.tensor_copy(fcT[:, :], f_bank[0][:, 3 * D:4 * D]).then_inc(ev_wq, 1)
            k_rows(2)
            k_rows(3)
            sums = t_bank[:, :].rearrange("p (a w) -> p a w", w=VW)

            def layernorm(k, count):
                b, second = count // 2, count % 2
                if k == 0 and not second:
                    dve.wait_ge(ps_fc, b + 1)
                    dve.wait_ge(resb, b + 1)
                    nc.vector.tensor_tensor(res[:, :, :].rearrange("p t c -> p (t c)"), f_bank[0][:, :],
                                            x_res[:, :, :].rearrange("p t c -> p (t c)"), ALU.add).then_inc(ln_step, 1)
                elif k == 0:
                    dve.wait_ge(ps_w3T, b + 1)
                    nc.vector.tensor_tensor(res[:, :, :].rearrange("p t c -> p (t c)"), t_bank[:, :],
                                            x1[:, :, :].rearrange("p t c -> p (t c)"), ALU.add).then_inc(ln_step, 1)
                elif k == 1:
                    dve.wait_ge(ln_step, 4 * count + 1)
                    for t in range(NT):
                        last = nc.vector.bn_stats(stats[:, t, :], res[:, t, :])
                    last.then_inc(ln_step, 1)
                elif k == 2:
                    dve.wait_ge(ln_step, 4 * count + 2)
                    for t in range(NT):
                        last = nc.vector.bn_aggr(mv[:, t, :], stats[:, t, :])
                    last.then_inc(ln_step, 1)
                elif k == 3:
                    dve.wait_ge(ln_step, 4 * count + 3)
                    nc.vector.tensor_scalar(rstd[:, 0, :], mv[:, :, 1], EPS, None, ALU.add).then_inc(ln_step, 1)
                else:
                    dve.wait_ge(rs_ok, count + 1)
                    if second:
                        wait(dve, st_out, 16 * b)
                    dst, done = ((x1, x1_ok), (y, y_ok))[second]
                    for t in range(NT):
                        last = nc.vector.tensor_scalar(dst[:, t, :], res[:, t, :], mv[:, t, 0:1], rstd[:, 1, t:t + 1],
                                                       ALU.subtract, ALU.mult)
                    last.then_inc(done, 1)

            def low_part(u):
                dve.wait_ge(ev_wt, u + 1)
                mx = nc.vector.tensor_reduce(wlow[:, u:u + 1], wt_dst(u, 1).bitcast(F32), AX.X, ALU.max,
                                             apply_absolute_value=True)
                if u == WT - 1:
                    mx.then_inc(lo_max, 1)

            for s, it in program(ALL):
                what = it[0]
                if what == "s":
                    mm = it[1]
                    m = BT * max(s, 0) + mm
                    c, qt = (m % GT) // NT, m % NT
                    g = m // GT
                    if m % GT == 0:
                        wait(dve, m_parts, g - 1)
                    dve.wait_ge(ps_s, m + 1)
                    nc.vector.tensor_reduce(negmax[:, g % 2, c, qt:qt + 1], s_bank[m % NS][:, :], AX.X,
                                            ALU.max, negate=True).then_inc(ev_s, 1)
                elif what == "split":
                    b, k, i = s + 1, it[1], it[2]
                    n = 2 * b + i
                    pt = parts[i]
                    A, Bs, C = ((0, 1, 2), (3, 4), 5) if i == 0 else ((0, 3, 5), (1, 4), 2)
                    if k == 0:
                        dve.wait_ge(ev_qk, n + 1)
                        if b:
                            for h in range(H):
                                dve.wait_ge(rep[h], 16 * 2 * b)
                        nc.vector.tensor_copy(pt[:, A[0], :], qk_f[i][:, :]).then_inc(qk_step[i], 1)
                    elif k == 1:
                        dve.wait_ge(qk_step[i], 3 * b + 1)
                        nc.vector.tensor_tensor(qk_r[i][:, :], qk_f[i][:, :], pt[:, A[0], :], ALU.subtract).then_inc(qk_step[i], 1)
                        for a in A[1:]:
                            nc.vector.tensor_copy(pt[:, a, :], pt[:, A[0], :])
                    elif k == 2:
                        dve.wait_ge(qk_step[i], 3 * b + 2)
                        nc.vector.tensor_copy(pt[:, Bs[0], :], qk_r[i][:, :]).then_inc(qk_step[i], 1)
                    else:
                        dve.wait_ge(qk_step[i], 3 * b + 3)
                        nc.vector.tensor_copy(pt[:, Bs[1], :], pt[:, Bs[0], :])
                        nc.vector.tensor_tensor(pt[:, C, :], qk_r[i][:, :], pt[:, Bs[0], :], ALU.subtract).then_inc(qk_parts[i], 1)
                elif what == "v_in":
                    b = max(s, 0)
                    dve.wait_ge(ps_v, b + 1)
                    if b == 0:
                        dve.wait_ge(ld_vb, 16 * NT)
                        dve.wait_ge(vzero, 2)
                    wait(dve, ps_pv, NG * NT * b)
                    nc.vector.tensor_tensor(v_sb[:, :, :, 0:HD].rearrange("p t h d -> p (t h) d"),
                                            f_bank[0][:, :].rearrange("p (a d) -> p a d", d=HD),
                                            vb[:, :, :].rearrange("p t (h d) -> p (t h) d", d=HD), ALU.add).then_inc(ev_v, 1)
                elif what == "oT_rec":
                    g = NG * s + it[1]
                    dve.wait_ge(ps_oT, g + 1)
                    nc.vector.reciprocal(rden[:, :], sums[:, :, HD]).then_inc(rd_oT, 1)
                elif what == "oT_mul":
                    g = NG * s + it[1]
                    j = g % NG
                    dve.wait_ge(rd_oT, g + 1)
                    if j == 0:
                        wait(dve, ps_aT, g // NG)
                    for t in range(NT):
                        last = nc.vector.tensor_tensor(
                            attn[:, t, GH * HD * j:GH * HD * (j + 1)].rearrange("p (c d) -> p c d", d=HD),
                            sums[:, GH * t:GH * (t + 1), 0:HD],
                            rden[:, GH * t:GH * (t + 1)].unsqueeze(2).broadcast_to([P, GH, HD]), ALU.mult)
                    last.then_inc(ev_oT, 1)
                elif what == "ln":
                    layernorm(it[1], it[2])
                elif what == "x1T_hi":
                    dve.wait_ge(ps_x1T, s)
                    wait(dve, ps_w2, NK * (s - 1))
                    nc.vector.tensor_copy(x1T[0][:, :], t_bank[:, :]).then_inc(hi_x1T, 1)
                elif what == "x1T_lo":
                    dve.wait_ge(hi_x1T, s)
                    nc.vector.tensor_tensor(x1T[1][:, :], t_bank[:, :], x1T[0][:, :].bitcast(F32), ALU.subtract).then_inc(ev_x1T, 1)
                elif what == "w12":
                    k = it[1]
                    n = NK * (s - 1) + k
                    dve.wait_ge(ps_w2, n + 1)
                    dve.wait_ge(ev_w1, n + 1)
                    wait(dve, lo0, n - 1)
                    nc.vector.scalar_tensor_tensor(hf[:, k % 2, :], w2_bank(s, k)[:, :], hs[:, 1, k:k + 1], silu[:, k % 2, :],
                                                   ALU.mult, ALU.mult).then_inc(ev_w2, 1)
                elif what == "w12_lo":
                    k = it[1]
                    dve.wait_ge(hi0, NK * (s - 1) + k + 1)
                    nc.vector.tensor_tensor(act0[1][:, k, :], hf[:, k % 2, :], act0[0][:, k, :].bitcast(F32),
                                            ALU.subtract).then_inc(lo0, 1)
                elif what == "w12_hi":
                    k = it[1]
                    n = NK * (s - 1) + k
                    dve.wait_ge(ev_w2, n + 1)
                    if k == 0:
                        wait(dve, ps_w3, s - 1)
                    nc.vector.tensor_copy(act0[0][:, k, :], hf[:, k % 2, :]).then_inc(hi0, 1)
                elif what == "h":
                    layer, k = it[1], it[2]
                    n = NK * (2 * (s - 1) + layer) + k
                    dve.wait_ge(ev_h, n + 1)
                    if k == 0 and layer == 0:
                        wait(dve, ps_h, 2 * NK * (s - 1))
                    elif k == 0:
                        wait(dve, ps_h, NK * (2 * (s - 1) + 1))
                    a = (act1, act2)[layer]
                    nc.vector.tensor_copy(a[0][:, k, :], gf[:, k % 2, :]).then_inc(hi_g, 1)
                    if s == B:
                        dve.wait_ge(hi_g, n + 1)
                        nc.vector.tensor_tensor(a[1][:, k, :], gf[:, k % 2, :], a[0][:, k, :].bitcast(F32),
                                                ALU.subtract).then_inc(lo_g, 1)
                elif what == "wt_lo":
                    u = it[1]
                    dve.wait_ge(hi_wt, u + 1)
                    nc.vector.tensor_tensor(wt_dst(u, 1), f_bank[0][:, :], wt_dst(u, 0).bitcast(F32), ALU.subtract).then_inc(ev_wt, 1)
                    if u:
                        low_part(u - 1)
                elif what == "w_low":
                    low_part(WT - 1)
                    dve.wait_ge(lo_max, 1)
                    nc.vector.tensor_reduce(wlow1[:, :], wlow[:, :], AX.X, ALU.max).then_inc(lo_max, 1)
                    dve.wait_ge(ps_low, 1)
                    nc.vector.tensor_reduce(wflag[:, :], f_bank[0][0:1, 0:P], AX.X, ALU.max).then_inc(low_ok, 1)

        @block.gpsimd
        def _(pool):
            nc.gpsimd.memset(ident[:, :], 0.0).then_inc(ids, 1)
            nc.gpsimd.memset(ident16[:, :], 0.0).then_inc(ids, 1)
            pool.wait_ge(ids, 2)
            for m in (ident, ident16):
                nc.gpsimd.affine_select(out=m[:, :], in_=m[:, :], compare_op=ALU.not_equal, fill=1.0, base=0,
                                        pattern=[[-1, P]], channel_multiplier=1).then_inc(ids, 1)
            pool.wait_ge(ids, 4)
            for j in range(NG):
                rows = stack[0][:, GH * j:GH * (j + 1), :].rearrange("p h n -> p (h n)").bitcast(F32)
                wait(pool, zeros, 2 * j)
                nc.gpsimd.memset(rows[32:64, :], 0.0).then_inc(zeros, 1)
                pool.wait_ge(zeros, 2 * j + 1)
                nc.gpsimd.memset(rows[64:P, :], 0.0).then_inc(zeros, 1)
            pool.wait_ge(zeros, 2 * NG)
            nc.gpsimd.memset(v_sb[:, :, :, :], 0.0).then_inc(vzero, 1)
            pool.wait_ge(vzero, 1)
            nc.gpsimd.memset(v_sb[:, :, :, HD:HD + 1], 1.0).then_inc(vzero, 1)

            nc.gpsimd.memset(mhalf[:, :], -0.5).then_inc(vzero, 1)

            def inv_sqrt(count):
                pool.wait_ge(ln_step, 4 * count + 4)
                if count == 0:
                    pool.wait_ge(vzero, 3)
                nc.gpsimd.tensor_tensor(rstd[:, 1, :], rstd[:, 0, :], mhalf[:, :], ALU.pow).then_inc(rs_ok, 1)

            for s, it in program(ALL):
                what = it[0]
                if what == "ln" and it[1] == 3:
                    inv_sqrt(it[2])
                elif what == "m_split":
                    g = NG * s + it[1] if s >= 0 else 0
                    pool.wait_ge(ev_s, GT * (g + 1))
                    wait(pool, ps_mT, g)
                    nm = negmax[:, g % 2]
                    nc.gpsimd.tensor_copy(mparts[:, 0, :, :], nm).then_inc(m_step, 1)
                    pool.wait_ge(m_step, 3 * g + 1)
                    nc.gpsimd.tensor_tensor(mres[:, :, :], nm, mparts[:, 0, :, :], ALU.subtract).then_inc(m_step, 1)
                    pool.wait_ge(m_step, 3 * g + 2)
                    nc.gpsimd.tensor_copy(mparts[:, 1, :, :], mres[:, :, :]).then_inc(m_step, 1)
                    pool.wait_ge(m_step, 3 * g + 3)
                    nc.gpsimd.tensor_tensor(mparts[:, 2, :, :], mres[:, :, :], mparts[:, 1, :, :],
                                            ALU.subtract).then_inc(m_parts, 1)
                elif what == "pv" and it[1] == 1 and it[2] == 0 and s < B:
                    if s == 0:
                        pool.wait_ge(ld_fcb, 16 * NT)
                    pool.wait_ge(ld_res, 16 * (s + 1))
                    nc.gpsimd.tensor_tensor(x_res[:, :, :], x_res[:, :, :], x_res[:, :, :], ALU.add).then_inc(res2, 1)
                    pool.wait_ge(res2, s + 1)
                    nc.gpsimd.tensor_tensor(x_res[:, :, :], x_res[:, :, :], fcb[:, :, :], ALU.add).then_inc(resb, 1)
                elif what == "w12_hi" and s < B:
                    k = it[1]
                    n = NK * (s - 1) + k
                    pool.wait_ge(hi0, n + 1)
                    nc.gpsimd.tensor_tensor(act0[1][:, k, :], hf[:, k % 2, :], act0[0][:, k, :].bitcast(F32),
                                            ALU.subtract).then_inc(lo0, 1)
                elif what == "h" and s < B:
                    layer, k = it[1], it[2]
                    n = NK * (2 * (s - 1) + layer) + k
                    pool.wait_ge(hi_g, n + 1)
                    a = (act1, act2)[layer]
                    nc.gpsimd.tensor_tensor(a[1][:, k, :], gf[:, k % 2, :], a[0][:, k, :].bitcast(F32),
                                            ALU.subtract).then_inc(lo_g, 1)


_INS = ['L0_attn_x', 'L0_attn_qkv_w', 'L0_attn_qkv_b', 'L0_attn_fc_w', 'L0_attn_fc_b', 'L0_ffn_w1_w', 'L0_ffn_w1_s',
        'L0_ffn_w2_w', 'L0_ffn_w2_s', 'L0_ffn_h1_w', 'L0_ffn_h1_s', 'L0_ffn_h2_w', 'L0_ffn_h2_s', 'L0_ffn_w3_w',
        'L0_ffn_w3_s']
_OUTS = [((4, 512, 128), 'float32')]


def kernel(**inputs):
    import numpy as _np
    import concourse.bacc as _bacc
    from concourse import mybir as _mybir
    from concourse.bass_utils import run_bass_kernel_spmd as _run

    nc = _bacc.Bacc("TRN2", target_bir_lowering=False, num_devices=1)
    arrays, args = {}, []
    for name in _INS:
        a = _np.ascontiguousarray(inputs[name])
        arrays[f"in_{name}_dram"] = a
        args.append(nc.dram_tensor(f"in_{name}_dram", a.shape, _mybir.dt.from_np(a.dtype), kind="ExternalInput").ap())
    for i, (shape, dtype) in enumerate(_OUTS):
        dt = _mybir.dt.from_np(_np.dtype(dtype))
        args.append(nc.dram_tensor(f"out_{i}_dram", shape, dt, kind="ExternalOutput").ap())
    post_ln_block_kernel(nc, *args)
    r = _run(nc, [arrays], core_ids=[0])
    got = tuple(r.results[0][f"out_{i}_dram"] for i in range(len(_OUTS)))
    return got[0]
```
